# Optimizing a Trainium2 kernel written in Bass

```python
import numpy as np
import jax
import jax.numpy as jnp

def _softmax(x, axis=-1):
    return jax.nn.softmax(x, axis=axis)

def _gelu(x):
    return jax.nn.gelu(x, approximate=True)

def _silu(x):
    return jax.nn.silu(x)

def _sigmoid(x):
    return jax.nn.sigmoid(x)

def _layernorm(x, axis=-1, eps=1e-05):
    m = jnp.mean(x, axis=axis, keepdims=True)
    v = jnp.var(x, axis=axis, keepdims=True)
    return (x - m) / jnp.sqrt(v + eps)

def _scatter_add(tgt, idx, src, axis=0):
    return tgt.at[idx].add(src)

def _segment_sum(src, seg, n):
    return jax.ops.segment_sum(src, seg, n)
kernel_name = 'mk_seq_postln_d1_jaxref_r4_d249bf'

def setup_inputs(seed: int=0):
    np.random.seed(seed)
    _w = jnp.asarray

    def _L0_attn_setup():
        import jax, jax.numpy as jnp
        import numpy as np
        E2M1_GRID = jnp.array([0.0, 0.5, 1.0, 1.5, 2.0, 3.0, 4.0, 6.0], dtype=jnp.float32)
        E2M1_MIDS = (E2M1_GRID[1:] + E2M1_GRID[:-1]) / 2.0
        FP4_MAX = 6.0
        FP8_E4M3_MAX = 448.0

        def nvfp4_quant_dequant(w):
            O, I = w.shape
            w16 = w.reshape(O, I // 128, 8, 16)
            amax128 = jnp.max(jnp.abs(w16), axis=(-2, -1))
            outer = amax128 / (FP4_MAX * FP8_E4M3_MAX)
            outer = jnp.where(outer > 0, outer, 1.0)
            amax16 = jnp.max(jnp.abs(w16), axis=-1)
            inner = amax16 / FP4_MAX / outer[..., None]
            inner = inner.astype(jnp.float8_e4m3fn).astype(jnp.float32)
            scale = outer[..., None] * inner
            safe = jnp.where(scale > 0, scale, 1.0)[..., None]
            code = w16 / safe
            a = jnp.abs(code)
            idx = jnp.searchsorted(E2M1_MIDS, a)
            q = E2M1_GRID[idx] * jnp.sign(code)
            return (q * scale[..., None]).reshape(O, I)
        key = jax.random.key(seed)
        k0, k1, k2 = jax.random.split(key, 3)
        B, S, H = (2, 512, 512)
        hidden_states = jax.random.normal(k0, (B, S, H), dtype=jnp.float32)
        w_qkv = jax.random.normal(k1, (3 * H, H), dtype=jnp.float32) * 0.023
        w_o = jax.random.normal(k2, (H, H), dtype=jnp.float32) * 0.023
        w_qkv = nvfp4_quant_dequant(w_qkv)
        w_o = nvfp4_quant_dequant(w_o)
        return {'hidden_states': hidden_states, 'w_qkv': w_qkv, 'w_o': w_o}
    _L0_attn_in = _L0_attn_setup()

    def _L0_ffn_setup():
        import jax, jax.numpy as jnp
        import numpy as np
        BLOCK_SIZE = 32
        HIDDEN_SIZE = 512
        MLP_DIM = 4096
        NVFP4_LUT = jnp.array([0.0, 0.5, 1.0, 1.5, 2.0, 3.0, 4.0, 6.0, 0.0, -0.5, -1.0, -1.5, -2.0, -3.0, -4.0, -6.0], dtype=jnp.float32)

        def dequant_nvfp4(W_packed, scales, block=BLOCK_SIZE):
            N = W_packed.shape[0]
            low = W_packed & 15
            high = W_packed >> 4 & 15
            idx = jnp.stack([low, high], axis=-1).reshape(N, -1)
            vals = NVFP4_LUT[idx]
            K = vals.shape[1]
            vals = vals.reshape(N, K // block, block) * scales[:, :, None]
            return vals.reshape(N, K)
        key = jax.random.key(seed)
        ks = jax.random.split(key, 7)
        x = jax.random.normal(ks[0], (4, 32, HIDDEN_SIZE), dtype=jnp.float32)
        gate_W_packed = jax.random.randint(ks[1], (MLP_DIM, HIDDEN_SIZE // 2), 0, 64, dtype=jnp.int32)
        gate_scales = jax.random.uniform(ks[2], (MLP_DIM, HIDDEN_SIZE // BLOCK_SIZE), dtype=jnp.float32) * 0.1 + 0.001
        up_W_packed = jax.random.randint(ks[3], (MLP_DIM, HIDDEN_SIZE // 2), 0, 64, dtype=jnp.int32)
        up_scales = jax.random.uniform(ks[4], (MLP_DIM, HIDDEN_SIZE // BLOCK_SIZE), dtype=jnp.float32) * 0.1 + 0.001
        down_W_packed = jax.random.randint(ks[5], (HIDDEN_SIZE, MLP_DIM // 2), 0, 64, dtype=jnp.int32)
        down_scales = jax.random.uniform(ks[6], (HIDDEN_SIZE, MLP_DIM // BLOCK_SIZE), dtype=jnp.float32) * 0.1 + 0.001
        return {'x': x, 'gate_W_packed': gate_W_packed, 'gate_scales': gate_scales, 'up_W_packed': up_W_packed, 'up_scales': up_scales, 'down_W_packed': down_W_packed, 'down_scales': down_scales}
    _L0_ffn_in = _L0_ffn_setup()
    _d = {'L0_attn_hidden_states': _L0_attn_in['hidden_states'], 'L0_attn_w_qkv': _L0_attn_in['w_qkv'], 'L0_attn_w_o': _L0_attn_in['w_o'], 'L0_ffn_gate_W_packed': _L0_ffn_in['gate_W_packed'], 'L0_ffn_gate_scales': _L0_ffn_in['gate_scales'], 'L0_ffn_up_W_packed': _L0_ffn_in['up_W_packed'], 'L0_ffn_up_scales': _L0_ffn_in['up_scales'], 'L0_ffn_down_W_packed': _L0_ffn_in['down_W_packed'], 'L0_ffn_down_scales': _L0_ffn_in['down_scales']}
    _x0 = _d['L0_attn_hidden_states']
    _d['L0_attn_hidden_states'] = jax.random.normal(jax.random.fold_in(jax.random.key(seed), 1), (8, 512, 512), dtype=_x0.dtype)
    del _x0
    return _d

def reference(L0_attn_hidden_states, L0_attn_w_qkv, L0_attn_w_o, L0_ffn_gate_W_packed, L0_ffn_gate_scales, L0_ffn_up_W_packed, L0_ffn_up_scales, L0_ffn_down_W_packed, L0_ffn_down_scales):

    def _L0_attn_ref(hidden_states, w_qkv, w_o):
        import jax, jax.numpy as jnp
        import numpy as np
        E2M1_GRID = jnp.array([0.0, 0.5, 1.0, 1.5, 2.0, 3.0, 4.0, 6.0], dtype=jnp.float32)
        E2M1_MIDS = (E2M1_GRID[1:] + E2M1_GRID[:-1]) / 2.0
        FP4_MAX = 6.0
        FP8_E4M3_MAX = 448.0

        def nvfp4_quant_dequant(w):
            O, I = w.shape
            w16 = w.reshape(O, I // 128, 8, 16)
            amax128 = jnp.max(jnp.abs(w16), axis=(-2, -1))
            outer = amax128 / (FP4_MAX * FP8_E4M3_MAX)
            outer = jnp.where(outer > 0, outer, 1.0)
            amax16 = jnp.max(jnp.abs(w16), axis=-1)
            inner = amax16 / FP4_MAX / outer[..., None]
            inner = inner.astype(jnp.float8_e4m3fn).astype(jnp.float32)
            scale = outer[..., None] * inner
            safe = jnp.where(scale > 0, scale, 1.0)[..., None]
            code = w16 / safe
            a = jnp.abs(code)
            idx = jnp.searchsorted(E2M1_MIDS, a)
            q = E2M1_GRID[idx] * jnp.sign(code)
            return (q * scale[..., None]).reshape(O, I)
        B, S, H = hidden_states.shape
        num_heads = 16
        head_dim = H // num_heads
        qkv = jnp.einsum('bsh,oh->bso', hidden_states, w_qkv)
        qkv = qkv.reshape(B, S, 3, num_heads, head_dim)
        qkv = jnp.transpose(qkv, (2, 0, 3, 1, 4))
        q, k, v = (qkv[0], qkv[1], qkv[2])
        scale = 1.0 / jnp.sqrt(jnp.float32(head_dim))
        scores = jnp.einsum('bhqd,bhkd->bhqk', q, k) * scale
        causal = jnp.tril(jnp.ones((S, S), dtype=bool))
        scores = jnp.where(causal, scores, jnp.finfo(scores.dtype).min)
        probs = jax.nn.softmax(scores, axis=-1)
        attn = jnp.einsum('bhqk,bhkd->bhqd', probs, v)
        attn = jnp.transpose(attn, (0, 2, 1, 3)).reshape(B, S, H)
        return jnp.einsum('bsh,oh->bso', attn, w_o)

    def _L0_ffn_ref(x, gate_W_packed, gate_scales, up_W_packed, up_scales, down_W_packed, down_scales):
        import jax, jax.numpy as jnp
        import numpy as np
        BLOCK_SIZE = 32
        HIDDEN_SIZE = 512
        MLP_DIM = 4096
        NVFP4_LUT = jnp.array([0.0, 0.5, 1.0, 1.5, 2.0, 3.0, 4.0, 6.0, 0.0, -0.5, -1.0, -1.5, -2.0, -3.0, -4.0, -6.0], dtype=jnp.float32)

        def dequant_nvfp4(W_packed, scales, block=BLOCK_SIZE):
            N = W_packed.shape[0]
            low = W_packed & 15
            high = W_packed >> 4 & 15
            idx = jnp.stack([low, high], axis=-1).reshape(N, -1)
            vals = NVFP4_LUT[idx]
            K = vals.shape[1]
            vals = vals.reshape(N, K // block, block) * scales[:, :, None]
            return vals.reshape(N, K)
        B, S, H = x.shape
        xt = x.reshape(B * S, H)
        Wg = dequant_nvfp4(gate_W_packed, gate_scales)
        Wu = dequant_nvfp4(up_W_packed, up_scales)
        Wd = dequant_nvfp4(down_W_packed, down_scales)
        gate = jnp.einsum('th,nh->tn', xt, Wg)
        up = jnp.einsum('th,nh->tn', xt, Wu)
        gelu = jnp.tanh(0.7978845608028654 * (gate + 0.044715 * gate ** 3)) * gate * 0.5 + gate * 0.5
        inter = gelu * up
        out = jnp.einsum('tn,hn->th', inter, Wd)
        return out.reshape(B, S, H)
    x = L0_attn_hidden_states
    x = _layernorm(x + _L0_attn_ref(x, L0_attn_w_qkv, L0_attn_w_o), axis=-1)
    x = _layernorm(x + _L0_ffn_ref(x, L0_ffn_gate_W_packed, L0_ffn_gate_scales, L0_ffn_up_W_packed, L0_ffn_up_scales, L0_ffn_down_W_packed, L0_ffn_down_scales), axis=-1)
    return x

_drawn_inputs = setup_inputs


def setup_inputs(seed=0):
    import zlib

    import numpy as np

    out = dict(_drawn_inputs(seed))
    spreads = {}
    factors = {}
    for name, (base, spread) in spreads.items():
        noise = np.random.default_rng([zlib.crc32(name.encode()), seed]).standard_normal(out[name].shape)
        drawn = base * np.exp(spread * noise) if base else spread * noise
        out[name] = jnp.asarray(drawn.astype(out[name].dtype))
    for name, factor in factors.items():
        out[name] = (out[name] * factor).astype(out[name].dtype)
    return out
```

```python
import concourse.bass as bass
from concourse import mybir

F32 = mybir.dt.float32
F32R = mybir.dt.float32r
I32 = mybir.dt.int32
F16 = mybir.dt.float16
ALU = mybir.AluOpType
ACT = mybir.ActivationFunctionType

P = 128
BATCH, SEQ, HID = 8, 512, 512
HEADS = 16
HD = HID // HEADS
MLP = 4096
EPS = 1e-5
SCALE = float(HD) ** -0.5
KC = HID // P
TT = SEQ // P
GROUPS = HEADS // 4
TOK = BATCH * SEQ
MASKED = -1e30
PCOL = [0, 128, 384, 768]
TCOL = [0, 512, 896, 1152]
PW = 1280


class Plan:

    def __init__(self, nc):
        self.nc, self.at, self.where = nc, (nc.sbuf_base + 63) // 64 * 64, {}

    def __call__(self, name, shape, dtype, over=None, skip=0):
        size = 4
        for n in shape[1:]:
            size *= n
        offset = self.where[over] + skip if over else self.at
        if not over:
            self.at += (size + 31) // 32 * 32
        self.where[name] = offset
        return self.nc.alloc_sbuf_tensor_at(name, shape, dtype, offset=offset)


def wait_apart(eng, passed, semaphore, value):
    eng.wait_ge(semaphore, value)
    eng.sem_inc(passed, 1)


def f32(ap):
    return ap.bitcast(F32)


def attention_phase(nc, bank, xT_dram, x_dram, wqkvT, woT, tri, ident_dram, x1_dram, x1T_dram, qk_dram):
    plan = Plan(nc)
    w_h = plan("w_h", [P, KC, 3 * HID], F32R)
    w_l = plan("w_l", [P, KC, 3 * HID], F32R)
    wo_h = plan("wo_h", [P, KC, HID], F32R)
    wo_l = plan("wo_l", [P, KC, HID], F32R)
    x_h = plan("x_h", [P, KC, SEQ], F32R)
    x_l = plan("x_l", [P, KC, SEQ], F32R)
    xs = plan("xs", [P, 2, SEQ], F32)
    qk_stage = plan("qk_stage", [P, 2, SEQ], F32)
    q_st = plan("q_st", [P, 2, 4, SEQ], F32R)
    k_st = plan("k_st", [P, 2, 4, SEQ], F32R)
    v_pad = plan("v_pad", [P, TT, HEADS, P], F32R)
    probs = plan("probs", [P, 4, PW], F32)
    w_stage = plan("w_stage", [P, 2, 4 * HID], F32, over="probs")
    pT_h = plan("pT_h", [P, PW], F32R)
    pT_l = plan("pT_l", [P, PW], F32R)
    y = plan("y", [P, TT, HID], F32, over="pT_h")
    lo_part = plan("lo_part", [64, SEQ], F32)
    a_sum = plan("a_sum", [P, SEQ], F32)
    a_h = plan("a_h", [P, KC, SEQ], F32R)
    a_l = plan("a_l", [P, KC, SEQ], F32R)
    mask = plan("mask", [P, SEQ], F32)
    ident = plan("ident", [P, P], F32)
    neg_max = plan("neg_max", [P, 4, TT], F32)
    row_sum = plan("row_sum", [P, 4, TT], F32)
    row_inv = plan("row_inv", [P, 4, TT], F32)
    stats = plan("stats", [P, TT, 6], F32)
    mean_var = plan("mean_var", [P, TT, 2], F32)
    var_eps = plan("var_eps", [P, TT], F32)
    std = plan("std", [P, TT], F32)
    rstd = plan("rstd", [P, TT], F32)
    assert plan.at <= nc.sbuf_usable_end, plan.at

    proj_bank, s_bank, t_bank, o_bank = bank[0:2], bank[2:4], bank[4:6], bank[6:8]

    sem = lambda name: nc.alloc_semaphore("a_" + name)
    const_loaded = sem("const_loaded")
    w_loaded = [sem("w_loaded0"), sem("w_loaded1")]
    w_high = sem("w_high")
    w_split = sem("w_split")
    v_zero = sem("v_zero")
    x_loaded = [sem("x_loaded0"), sem("x_loaded1")]
    x_high = sem("x_high")
    x_split = sem("x_split")
    proj_done, proj_high, proj_free = sem("proj_done"), sem("proj_high"), sem("proj_free")
    qk_written = sem("qk_written")
    stack_loaded = sem("stack_loaded")
    s_done, s_masked = sem("s_done"), sem("s_masked")
    exp_done, inv_done, norm_done = sem("exp_done"), sem("inv_done"), sem("norm_done")
    t_done, t_high, t_free = sem("t_done"), sem("t_high"), sem("t_free")
    pv_done, o_low, o_free = sem("pv_done"), sem("o_low"), sem("o_free")
    a_high, a_split = sem("a_high"), sem("a_split")
    y_loaded, y_stat, y_agg = sem("y_loaded"), sem("y_stat"), sem("y_agg")
    var_done, std_done, rstd_done, x1_done = sem("var_done"), sem("std_done"), sem("rstd_done"), sem("x1_done")
    x1_stored = sem("x1_stored")
    x1T_stored = sem("x1T_stored")
    passed = sem("passed")

    PRE, PER = 6, 16
    STORED_CREDIT = 16
    QK0, VN, WO = 6, 8, 12
    t_use = lambda b, s, k: b * 68 + (4 * s + k)
    x1T_use = lambda b, t: b * 68 + (64 + t)

    X1T_SLOTS = {0: [0], 1: [1], 2: [2, 3]}

    def batches(eng, body):
        body(0, True, False)
        with eng.Fori(1, BATCH - 1) as b:
            body(b, False, False)
        body(BATCH - 1, False, True)

    block = nc.Block()
    with block as block:

        @block.sync
        def _(sp):
            sp.dma_start(mask[:], tri).then_inc(const_loaded, 16)
            sp.dma_start(ident[:], ident_dram).then_inc(const_loaded, 16)
            for c in range(KC):
                if c >= 2:
                    sp.wait_ge(w_split, 2 * (c - 1))
                sp.dma_start(w_stage[:, c % 2, 0:3 * HID], wqkvT[c * P:(c + 1) * P, :]).then_inc(w_loaded[c % 2], 16)
                sp.dma_start(w_stage[:, c % 2, 3 * HID:], woT[c * P:(c + 1) * P, :]).then_inc(w_loaded[c % 2], 16)

            def load_x(b, c):
                sp.wait_ge(x_split, b * KC + max(c - 1, 0))
                sp.dma_start(xs[:, c % 2, :], xT_dram[c * P:(c + 1) * P, bass.ts(b, SEQ)]).then_inc(x_loaded[c % 2], 16)

            def stack(use, b, c, which):
                n = (b * GROUPS + c) * 2 + which
                sp.wait_ge(proj_free, use + 3)
                sp.dma_start(qk_dram[which], qk_stage[:]).then_inc(qk_written, 16)
                sp.wait_ge(qk_written, n * 16 + 16)
                dst = (q_st, k_st)[which]
                for j in range(4):
                    part = j % 2 if which == 0 else j // 2
                    src = qk_dram[which][:, part, :].rearrange("(g p) t -> p g t", g=4)
                    sp.dma_start(f32(dst[32 * j:32 * j + 32, c % 2, :, :]), src).then_inc(stack_loaded, 16)
                wait_apart(sp, passed, stack_loaded, n * 64 + 64)

            def store_x1T(b, t):
                sp.wait_ge(t_free, x1T_use(b, t) + 3)
                tok = b * SEQ + t * P
                for part in range(2):
                    sp.dma_start(
                        x1T_dram[part].rearrange("(c p) t -> p c t", p=P)[:, :, bass.ds(tok, P)],
                        xs[:, part, :].rearrange("p (c t) -> p c t", c=KC)).then_inc(x1T_stored, 16)

            for c in range(KC):
                load_x(0, c)
            stack(0, 0, 0, 0)
            stack(1, 0, 0, 1)

            def body(b, first, last):
                base = b * PER + PRE
                for s in range(HEADS + 4):
                    if s in (0, 1, 4, 5, 8, 9):
                        c = s // 4 + 1
                        if c >= 2:
                            wait_apart(sp, passed, s_done, (b * HEADS + 4 * (c - 1)) * TT)
                        stack(base + (s // 4 * 2 + s % 4), b, c, s % 4)
                    for t in X1T_SLOTS.get(s, []):
                        if not first:
                            store_x1T(b - 1, t)
                    if s == 10 and not last:
                        if not first:
                            sp.wait_ge(x1T_stored, b * (TT * 32) + STORED_CREDIT)
                        for k in range(KC):
                            load_x(b + 1, k)
                    if s == 16 and not last:
                        wait_apart(sp, passed, s_done, (b * HEADS + 12) * TT)
                        stack(base + QK0, b + 1, 0, 0)
                        stack(base + (QK0 + 1), b + 1, 0, 1)
                sp.wait_ge(pv_done, (b * HEADS + HEADS) * TT)
                sp.dma_start(y[:], x_dram[bass.ts(b, SEQ), :].rearrange("(t p) h -> p t h", p=P)).then_inc(y_loaded, 16)
                sp.wait_ge(x1_done, b * TT + TT)
                sp.dma_start(x1_dram[bass.ts(b, SEQ), :].rearrange("(t p) h -> p t h", p=P), y[:]).then_inc(x1_stored, 16)

            batches(sp, body)
            for t in range(TT):
                store_x1T(BATCH - 1, t)
            sp.wait_ge(x1_stored, BATCH * 16)
            sp.wait_ge(x1T_stored, BATCH * TT * 32 + STORED_CREDIT)

        @block.tensor
        def _(pe):
            def three(out, ah, al, bh, bl, at, bt):
                for c in range(KC):
                    pe.matmul(out, at(ah, c), bt(bh, c), start=(c == 0), stop=False)
                    pe.matmul(out, at(ah, c), bt(bl, c), start=False, stop=False)
                    last = pe.matmul(out, at(al, c), bt(bh, c), start=False, stop=(c == KC - 1))
                return last

            def project_qk(use, which, c):
                pe.wait_ge(proj_free, use + 1)
                col = which * HID + c * P
                out = proj_bank[which % 2][:, :]
                three(out, w_h, w_l, x_h, x_l, lambda w, k: w[:, k, col:col + P],
                      lambda x, k: x[:, k, :]).then_inc(proj_done, 1)

            def project_v(use, t):
                pe.wait_ge(proj_free, use + 1)
                out = proj_bank[t % 2][:, :]
                three(out, x_h, x_l, w_h, w_l, lambda x, k: x[:, k, t * P:(t + 1) * P],
                      lambda w, k: w[:, k, 2 * HID:3 * HID]).then_inc(proj_done, 1)

            def project_out(use, t):
                pe.wait_ge(proj_free, use + 1)
                out = proj_bank[t % 2][:, :]
                three(out, a_h, a_l, wo_h, wo_l, lambda a, k: a[:, k, t * P:(t + 1) * P],
                      lambda w, k: w[:, k, :]).then_inc(proj_done, 1)

            def scores(b, s, k):
                use = (b * HEADS + s) * TT + k
                pe.wait_ge(s_masked, use + 1)
                g, st = s % 4, s // 4 % 2
                n = P * (k + 1)
                pe.matmul(s_bank[k % 2][:, 0:n], q_st[:, st, g, k * P:(k + 1) * P], k_st[:, st, g, 0:n],
                          start=True, stop=True).then_inc(s_done, 1)

            def transpose_probs(b, s, k):
                if k == 0:
                    pe.wait_ge(norm_done, (b * HEADS + s) * TT + TT)
                pe.wait_ge(t_free, t_use(b, s, k) + 1)
                for i in range(k, TT):
                    last = pe.transpose(t_bank[k % 2][:, (i - k) * P:(i - k + 1) * P],
                                        probs[:, s % 4, PCOL[i] + k * P:PCOL[i] + (k + 1) * P], ident[:])
                last.then_inc(t_done, 1)

            def values(b, s, k):
                pe.wait_ge(t_free, t_use(b, s, k) + 3)
                if s % 2 == 0 and k == 0:
                    pe.wait_ge(o_free, b * 8 + (s // 2 + 1))
                n = SEQ - k * P
                out = o_bank[s // 2 % 2][:, k * P:SEQ]
                pe.matmul(out, v_pad[:, k, s, :], pT_h[:, TCOL[k]:TCOL[k] + n],
                          start=(s % 2 == 0 and k == 0), stop=False, skip_group_check=True)
                last = pe.matmul(out, v_pad[:, k, s, :], pT_l[:, TCOL[k]:TCOL[k] + n],
                                 start=False, stop=(s % 2 == 1 and k == TT - 1), skip_group_check=True)
                last.then_inc(pv_done, 1)

            def transpose_x1(b, t):
                pe.wait_ge(x1_done, b * TT + t + 1)
                pe.wait_ge(t_free, x1T_use(b, t) + 1)
                for c in range(KC):
                    first = c // 2 * 256 + c % 2
                    last = pe.transpose(t_bank[t % 2][:, c * P:(c + 1) * P], y[:, t, first:first + 255:2], ident[:])
                last.then_inc(t_done, 1)

            pe.wait_ge(w_split, 2 * KC)
            pe.wait_ge(x_split, KC)
            project_qk(0, 0, 0)
            project_qk(1, 1, 0)
            for t in range(TT):
                project_v(2 + t, t)
            pe.wait_ge(const_loaded, 32)
            pe.wait_ge(proj_free, PRE + 2)

            def body(b, first, last):
                base = b * PER + PRE
                for s in range(HEADS + 4):
                    if s < HEADS and s % 4 == 0:
                        pe.wait_ge(stack_loaded, (b * GROUPS + s // 4 + 1) * 128)
                    if s == 4 and not first:
                        pe.wait_ge(proj_free, base + 2)
                    for k in range(TT):
                        if s < HEADS:
                            scores(b, s, k)
                        if 4 <= s:
                            values(b, s - 4, k)
                        if 3 <= s < HEADS + 3:
                            transpose_probs(b, s - 3, k)
                    for t in X1T_SLOTS.get(s, []):
                        if not first:
                            transpose_x1(b - 1, t)
                    if s in (0, 1, 4, 5, 8, 9):
                        project_qk(base + (s // 4 * 2 + s % 4), s % 4, s // 4 + 1)
                    if s in (16, 17) and not last:
                        if s == 16:
                            pe.wait_ge(x_split, b * KC + 2 * KC)
                        project_qk(base + (QK0 + s - 16), s - 16, 0)
                if not last:
                    for t in range(TT):
                        project_v(base + (VN + t), t)
                pe.wait_ge(a_split, b * GROUPS + GROUPS)
                for t in range(TT):
                    project_out(base + ((WO if not last else QK0) + t), t)

            batches(pe, body)
            for t in range(TT):
                transpose_x1(BATCH - 1, t)

        @block.scalar
        def _(act):
            def copy(out, in_):
                return act.activation(out, in_, ACT.Copy)

            for c in range(KC):
                act.wait_ge(w_loaded[c % 2], 32 * (c // 2 + 1))
                copy(w_h[:, c, :], w_stage[:, c % 2, 0:3 * HID]).then_inc(w_high, 1)
                copy(wo_h[:, c, :], w_stage[:, c % 2, 3 * HID:]).then_inc(w_high, 1)

            def x_part(b, c):
                act.wait_ge(x_loaded[c % 2], b * 32 + (c // 2 * 16 + 16))
                copy(x_h[:, c, :], xs[:, c % 2, :]).then_inc(x_high, 1)

            def qk_part(use, b, c, which):
                act.wait_ge(proj_done, use + 1)
                n = (b * GROUPS + c) * 2 + which
                act.wait_ge(qk_written, n * 16)
                copy(qk_stage[:, 0, :].bitcast(F32R), proj_bank[which][:, :]).then_inc(proj_high, 1)

            def v_part(use, t):
                act.wait_ge(proj_done, use + 1)
                v = proj_bank[t % 2][:, :].rearrange("p (g e d) -> p e g d", e=2, d=HD)
                dst = v_pad[:, t, :, :].rearrange("p (g e) n -> p e g n", e=2)
                copy(dst[:, 0, :, 0:HD], v[:, 0, :, :])
                copy(dst[:, 1, :, HD:2 * HD], v[:, 1, :, :]).then_inc(proj_high, 1)

            for c in range(KC):
                x_part(0, c)
            qk_part(0, 0, 0, 0)
            qk_part(1, 0, 0, 1)
            act.wait_ge(v_zero, 1)
            for t in range(TT):
                v_part(2 + t, t)

            def body(b, first, last):
                base = b * PER + PRE
                for s in range(HEADS + 5):
                    for k in range(TT):
                        if 1 <= s < HEADS + 1:
                            h, n = s - 1, P * (k + 1)
                            act.wait_ge(s_masked, (b * HEADS + h) * TT + k + 3)
                            p = probs[:, h % 4, PCOL[k]:PCOL[k] + n]
                            act.activation(p, p, ACT.Exp, bias=neg_max[:, h % 4, k:k + 1], scale=-1.0,
                                           accum_out=row_sum[:, h % 4, k:k + 1]).then_inc(exp_done, 1)
                        if 3 <= s < HEADS + 3:
                            h, n = s - 3, SEQ - k * P
                            act.wait_ge(t_done, t_use(b, h, k) + 1)
                            if h >= 1:
                                act.wait_ge(pv_done, (b * HEADS + h - 1) * TT + (k + 1))
                            if h == 0 and not first:
                                act.wait_ge(x1_stored, b * 16)
                            copy(pT_h[:, TCOL[k]:TCOL[k] + n], t_bank[k % 2][:, 0:n]).then_inc(t_high, 1)
                        if k == 0 and s >= 6 and s % 2 == 0:
                            low_half(b, (s - 6) // 2)
                    for t in X1T_SLOTS.get(s, []):
                        if not first:
                            x1T_high(b - 1, t)
                    if s >= 8 and s % 4 == 0:
                        group_high(b, (s - 8) // 4)
                    if s in (0, 1, 4, 5, 8, 9):
                        qk_part(base + (s // 4 * 2 + s % 4), b, s // 4 + 1, s % 4)
                    if 11 <= s < 15 and not last:
                        if s == 11:
                            act.wait_ge(proj_done, base + 6)
                        x_part(b + 1, s - 11)
                    if s in (16, 17) and not last:
                        qk_part(base + (QK0 + s - 16), b + 1, 0, s - 16)
                if not last:
                    act.wait_ge(pv_done, (b * HEADS + HEADS) * TT)
                    for t in range(TT):
                        v_part(base + (VN + t), t)
                act.wait_ge(var_done, b + 1)
                act.activation(std[:, :], var_eps[:, :], ACT.Sqrt).then_inc(std_done, 1)

            def x1T_high(b, t):
                act.wait_ge(t_done, x1T_use(b, t) + 1)
                act.wait_ge(x1T_stored, (b * TT + t) * 32 + STORED_CREDIT)
                copy(xs[:, 0, :].bitcast(F32R), t_bank[t % 2][:, :]).then_inc(t_high, 1)

            def low_half(b, p):
                act.wait_ge(pv_done, (b * HEADS + 2 * p + 2) * TT)
                act.wait_ge(o_free, b * 8 + p + 2)
                copy(lo_part[:, :], o_bank[p % 2][64:P, :]).then_inc(o_low, 1)

            def group_high(b, c):
                act.wait_ge(o_free, b * 8 + 2 * c + 4)
                if c == 0:
                    act.wait_ge(proj_done, b * PER + PRE)
                copy(a_h[:, c, :], a_sum[:, :]).then_inc(a_high, 1)

            batches(act, body)
            for t in range(TT):
                x1T_high(BATCH - 1, t)

        @block.vector
        def _(dve):
            def low(out, whole, high):
                return dve.tensor_tensor(out, whole, high, ALU.subtract)

            dve.sem_inc(proj_free, 2)
            dve.sem_inc(t_free, 2)
            dve.sem_inc(s_masked, 2)
            dve.sem_inc(o_free, 2)
            dve.sem_inc(x1T_stored, STORED_CREDIT)
            dve.memset(f32(v_pad[:]), 0.0).then_inc(v_zero, 1)
            for c in range(KC):
                dve.wait_ge(w_high, 2 * c + 1)
                low(w_l[:, c, :], w_stage[:, c % 2, 0:3 * HID], f32(w_h[:, c, :])).then_inc(w_split, 1)
                dve.wait_ge(w_high, 2 * c + 2)
                low(wo_l[:, c, :], w_stage[:, c % 2, 3 * HID:], f32(wo_h[:, c, :])).then_inc(w_split, 1)

            def x_part(b, c):
                dve.wait_ge(x_high, b * KC + c + 1)
                low(x_l[:, c, :], xs[:, c % 2, :], f32(x_h[:, c, :])).then_inc(x_split, 1)

            def qk_part(high, which):
                dve.wait_ge(proj_high, high)
                low(qk_stage[:, 1, :].bitcast(F32R), proj_bank[which][:, :], qk_stage[:, 0, :]).then_inc(proj_free, 1)

            def v_part(high, t):
                dve.wait_ge(proj_high, high)
                v = proj_bank[t % 2][:, :].rearrange("p (g e d) -> p e g d", e=2, d=HD)
                dst = v_pad[:, t, :, :].rearrange("p (g e) n -> p e g n", e=2)
                low(dst[:, 0, :, 64:64 + HD], v[:, 0, :, :], f32(dst[:, 0, :, 0:HD]))
                low(dst[:, 1, :, 64 + HD:P], v[:, 1, :, :], f32(dst[:, 1, :, HD:2 * HD])).then_inc(proj_free, 1)

            for c in range(KC):
                x_part(0, c)
            qk_part(1, 0)
            qk_part(2, 1)
            for t in range(TT):
                v_part(3 + t, t)
            dve.wait_ge(const_loaded, 32)

            def pair_sum(b, p):
                dve.wait_ge(o_low, b * 8 + p + 1)
                if p % 2 == 0:
                    dve.wait_ge(a_high, b * GROUPS + p // 2)
                r = 64 * (p % 2)
                dve.tensor_tensor(a_sum[r:r + 64, :], o_bank[p % 2][0:64, :], lo_part[:, :],
                                  ALU.add).then_inc(o_free, 1)

            def group_low(b, c):
                dve.wait_ge(a_high, b * GROUPS + c + 1)
                low(a_l[:, c, :], a_sum[:, :], f32(a_h[:, c, :])).then_inc(a_split, 1)

            def x1T_low(b, t):
                dve.wait_ge(t_high, x1T_use(b, t) + 1)
                low(xs[:, 1, :].bitcast(F32R), t_bank[t % 2][:, :], xs[:, 0, :]).then_inc(t_free, 1)

            def body(b, first, last):
                high = b * 12 + PRE
                for s in range(HEADS + 5):
                    if 2 <= s < HEADS + 2:
                        h = s - 2
                        dve.wait_ge(exp_done, (b * HEADS + h) * TT + TT)
                        dve.reciprocal(row_inv[:, h % 4, :], row_sum[:, h % 4, :]).then_inc(inv_done, 1)
                    for k in range(TT):
                        if s < HEADS:
                            n = P * (k + 1)
                            if k == 0 and (s >= 4 or not first):
                                dve.wait_ge(t_done, t_use(b, s - 4, TT) if s >= 4 else t_use(b - 1, HEADS + s - 4, TT))
                            wait_apart(dve, passed, s_done, (b * HEADS + s) * TT + k + 1)
                            dve.tensor_tensor_reduce(
                                probs[:, s % 4, PCOL[k]:PCOL[k] + n], s_bank[k % 2][:, 0:n], mask[:, SEQ - n:SEQ],
                                -SCALE, 3.0e38, ALU.add, ALU.min, neg_max[:, s % 4, k:k + 1]).then_inc(s_masked, 1)
                        if 3 <= s < HEADS + 3:
                            h, n = s - 3, SEQ - k * P
                            dve.wait_ge(t_high, t_use(b, h, k) + 1)
                            low(pT_l[:, TCOL[k]:TCOL[k] + n], t_bank[k % 2][:, 0:n],
                                f32(pT_h[:, TCOL[k]:TCOL[k] + n])).then_inc(t_free, 1)
                        if k == 0 and s >= 6 and s % 2 == 0:
                            pair_sum(b, (s - 6) // 2)
                    for t in X1T_SLOTS.get(s, []):
                        if not first:
                            x1T_low(b - 1, t)
                    if s >= 8 and s % 4 == 0:
                        group_low(b, (s - 8) // 4)
                    if s in (0, 1, 4, 5, 8, 9):
                        qk_part(high + (s // 4 * 2 + s % 4 + 1), s % 4)
                    if 11 <= s < 15 and not last:
                        x_part(b + 1, s - 11)
                    if s in (16, 17) and not last:
                        qk_part(high + (7 + s - 16), s - 16)
                if not last:
                    for t in range(TT):
                        v_part(high + (9 + t), t)
                base = b * PER + PRE + (WO if not last else QK0)
                dve.wait_ge(y_loaded, b * 16 + 16)
                for t in range(TT):
                    dve.wait_ge(proj_done, base + (t + 1))
                    dve.tensor_tensor(y[:, t, :], proj_bank[t % 2][:, :], y[:, t, :], ALU.add)\
                        .then_inc(proj_free, 1)
                    dve.wait_ge(proj_free, base + (t + 3))
                    dve.bn_stats(stats[:, t, :], y[:, t, :]).then_inc(y_stat, 1)
                    wait_apart(dve, passed, y_stat, b * TT + t + 1)
                    dve.bn_aggr(mean_var[:, t, :], stats[:, t, :]).then_inc(y_agg, 1)
                dve.wait_ge(y_agg, b * TT + TT)
                dve.tensor_scalar(var_eps[:, :], mean_var[:, :, 1], EPS, None, ALU.add).then_inc(var_done, 1)
                dve.wait_ge(std_done, b + 1)
                dve.reciprocal(rstd[:, :], std[:, :]).then_inc(rstd_done, 1)
                dve.wait_ge(rstd_done, b + 1)
                for t in range(TT):
                    dve.tensor_scalar(y[:, t, :], y[:, t, :], mean_var[:, t, 0:1], rstd[:, t:t + 1],
                                      ALU.subtract, ALU.mult).then_inc(x1_done, 1)

            batches(dve, body)
            for t in range(TT):
                x1T_low(BATCH - 1, t)

        @block.gpsimd
        def _(pool):
            def body(b, first, last):
                for h in range(HEADS):
                    wait_apart(pool, passed, inv_done, b * HEADS + h + 1)
                    for k in range(TT):
                        p = probs[:, h % 4, PCOL[k]:PCOL[k] + P * (k + 1)]
                        pool.tensor_scalar(p, p, row_inv[:, h % 4, k:k + 1], 1.0, ALU.mult,
                                           ALU.mult).then_inc(norm_done, 1)

            with pool.Fori(0, BATCH) as b:
                body(b, False, False)


TILE = 512
SUPER = 2048
NS = TOK // SUPER
ST = SUPER // TILE
SUB = TILE // P
GW = 256
NG = MLP // GW
STEPS = NG * ST
UNITS = 3
BLOCK = 32
C1, C2 = 0.7978845608028654, 0.044715


def feed_forward_phase(nc, bank, x1_dram, x1T_dram, packed, scales, out_dram):
    plan = Plan(nc)
    x_h = plan("bx_h", [P, KC, SUPER], F32R)
    x_l = plan("bx_l", [P, KC, SUPER], F32R)
    acc = plan("acc", [P, SUPER // P, HID], F32)
    wg = [plan(f"wg_{n}", [P, 2, KC, GW], F32R) for n in "hl"]
    wu = [plan(f"wu_{n}", [P, 2, KC, GW], F32R) for n in "hl"]
    wd = [plan(f"wd_{n}", [P, 2, 2, HID], F32R) for n in "hl"]
    inter = [plan(f"inter_{n}", [P, 2, 2, TILE], F32R) for n in "hl"]
    hid = plan("hid", [P, 2, TILE], F32)
    codes = plan("codes", [P, 2, 512], I32)
    scale = plan("scale", [P, 2, 512], F32)
    bits_a = plan("bits_a", [P, 512], I32)
    bits_b = plan("bits_b", [P, 512], I32)
    w32 = plan("w32", [P, 2, 512], F32)
    stats = plan("bstats", [P, SUPER // P, 6], F32)
    mean_var = plan("bmean_var", [P, SUPER // P, 2], F32)
    var_eps = plan("bvar_eps", [P, SUPER // P], F32)
    std = plan("bstd", [P, SUPER // P], F32)
    rstd = plan("brstd", [P, SUPER // P], F32)
    neg_mean = plan("neg_mean", [P, SUPER // P], F32)
    assert plan.at <= nc.sbuf_usable_end, plan.at

    g_bank, u_bank, d_bank = bank[0:2], bank[2:4], bank[4:8]

    sem = lambda name: nc.alloc_semaphore("b_" + name)
    x_loaded = [sem(f"x_loaded{t}") for t in range(ST)]
    acc_loaded = [sem(f"acc_loaded{t}") for t in range(ST)]
    unit_loaded = [sem("unit_loaded0"), sem("unit_loaded1")]
    bit_step = sem("bit_step")
    w_made, w_high, w_split = sem("w_made"), sem("w_high"), sem("w_split")
    g_done, u_done = sem("g_done"), sem("u_done")
    square_done, poly_done, tanh_done = sem("square_done"), sem("poly_done"), sem("tanh_done")
    gelu_done, hid_done = sem("gelu_done"), sem("hid_done")
    inter_high, inter_split = sem("inter_high"), sem("inter_split")
    d_done, d_added = sem("d_done"), sem("d_added")
    stat_done, agg_done = sem("stat_done"), sem("agg_done")
    var_done, std_done, rstd_done = sem("var_done"), sem("std_done"), sem("rstd_done")
    out_made = sem("out_made")
    passed = sem("passed")
    out_stored = [sem(f"out_stored{t}") for t in range(ST)]

    U_CREDIT = 8
    HID_CREDIT = 2
    SPLIT_CREDIT = 2
    ADD_CREDIT = 4
    OUT_CREDIT = 16
    D_CREDIT = 5
    W_CREDIT = 4
    SPLITW_CREDIT = 2
    U2 = 2 * UNITS

    def steps(eng, tail, body):
        with eng.Fori(0, NS) as st:
            for j in range(8):
                body(st, 0, st * (NG // 2), st * STEPS, j, True)
            with eng.Fori(1, NG // 2) as it:
                for j in range(8):
                    body(st, it * 2, st * (NG // 2) + it, st * STEPS + it * 8, j, False)
            tail(st)

    def weight_part(part, u, w, n):
        if u == 2:
            return wd[part][:, w, n, :]
        return (wg, wu)[u][part][:, w, n:KC:2, :]

    def half(ap, u):
        return ap if u == 2 else ap.rearrange("p (c n) -> p c n", c=2)

    block = nc.Block()
    with block as block:

        @block.sync
        def _(sp):
            def load_x(st, t):
                sp.wait_ge(u_done, st * (2 * STEPS) + (2 * t + 2))
                for part, dst in enumerate((x_h, x_l)):
                    src = x1T_dram[part].rearrange("(c p) t -> p c t", p=P)[:, :, bass.ds(st * SUPER + t * TILE, TILE)]
                    sp.dma_start(f32(dst[:, :, t * TILE:(t + 1) * TILE]), src).then_inc(x_loaded[t], 16)

            def load_acc(st, t):
                sp.wait_ge(out_stored[t], st * 16 + OUT_CREDIT)
                src = x1_dram[bass.ds(st * SUPER + t * TILE, TILE), :].rearrange("(a p) h -> p a h", p=P)
                sp.dma_start(acc[:, t * SUB:(t + 1) * SUB, :], src).then_inc(acc_loaded[t], 16)

            def load_unit(number, group, u, parity):
                sp.wait_ge(w_made, number * 2 + 2)
                loaded = unit_loaded[parity]
                if u < 2:
                    cols = bass.ts(group, GW)
                    sp.dma_start(half(codes[:, parity, :], u),
                                 packed[u][:, cols].rearrange("(c p) n -> p c n", p=P)).then_inc(loaded, 16)
                    for c in range(2):
                        src = scales[u][c * 8:(c + 1) * 8, cols].unsqueeze(1).broadcast_to([8, 16, GW])
                        sp.dma_start(scale[:, parity, c * GW:(c + 1) * GW], src).then_inc(loaded, 16)
                else:
                    sp.dma_start(codes[:, parity, :], packed[2][bass.ts(group, P), :]).then_inc(loaded, 16)
                    src = scales[2][bass.ts(group, 8), :].unsqueeze(1).broadcast_to([8, 16, HID])
                    sp.dma_start(scale[:, parity, :], src).then_inc(loaded, 32)

            for u in range(UNITS):
                load_unit(u, 0, u, u % 2)

            def body(st, group, pairs, all_steps, j, first):
                if first and j == 0:
                    for t in range(ST):
                        load_x(st, t)
                        load_acc(st, t)
                g, u = j // ST, j % ST
                if u < UNITS:
                    load_unit(pairs * (2 * UNITS) + ((g + 1) * UNITS + u), (group + (g + 1)) % NG, u, (g + 1 + u) % 2)

            def tail(st):
                for t in range(ST):
                    sp.wait_ge(out_made, st * (SUPER // P) + (t + 1) * SUB)
                    dst = out_dram[bass.ds(st * SUPER + t * TILE, TILE), :].rearrange("(a p) h -> p a h", p=P)
                    sp.dma_start(dst, acc[:, t * SUB:(t + 1) * SUB, :]).then_inc(out_stored[t], 16)

            steps(sp, tail, body)
            for t in range(ST):
                sp.wait_ge(out_stored[t], NS * 16 + OUT_CREDIT)

        @block.tensor
        def _(pe):
            def three(out, a, b, c, count, at, bt):
                pe.matmul(out, at(a[0]), bt(b[0]), start=(c == 0), stop=False)
                pe.matmul(out, at(a[0]), bt(b[1]), start=False, stop=False)
                return pe.matmul(out, at(a[1]), bt(b[0]), start=False, stop=(c == count - 1))

            def gate_up(step, w, t):
                for m in range(2):
                    pe.wait_ge(hid_done, step * 2 + (m + 1))
                    for weights, out, done in ((wg, g_bank[m], g_done), (wu, u_bank[m], u_done)):
                        for c in range(KC):
                            last = three(out[:, :], weights, (x_h, x_l), c, KC,
                                         lambda x: x[:, w, c, m * P:(m + 1) * P],
                                         lambda x: x[:, c, t * TILE:(t + 1) * TILE])
                        last.then_inc(done, 1)

            def down(step, w, parity):
                pe.wait_ge(inter_split, step * 2 + (2 + SPLIT_CREDIT))
                for q in range(SUB):
                    pe.wait_ge(d_added, step * SUB + (q + 1))
                    for m in range(2):
                        last = three(d_bank[q][:, :], inter, wd, m, 2,
                                     lambda x: x[:, parity, m, q * P:(q + 1) * P],
                                     lambda x: x[:, w, m, :])
                    last.then_inc(d_done, 1)

            def body(st, group, pairs, all_steps, j, first):
                g, t = j // ST, j % ST
                if first and g == 0:
                    pe.wait_ge(x_loaded[t], st * 32 + 32)
                if t == 0:
                    pe.wait_ge(w_split, pairs * (2 * U2) + (g * U2 + 4 + SPLITW_CREDIT))
                gate_up(all_steps + j, g, t)
                if not (first and j == 0):
                    if t == 1:
                        pe.wait_ge(w_split, pairs * (2 * U2) + (g * U2 + 6 + SPLITW_CREDIT))
                    down(all_steps + (j - 1), (j - 1) // ST % 2, (j - 1) % 2)

            def tail(st):
                down(st * STEPS + (STEPS - 1), 1, 1)

            steps(pe, tail, body)

        @block.scalar
        def _(act):
            def weight_high(number, u, w):
                for n in range(2):
                    act.wait_ge(w_made, number * 2 + (n + 1 + W_CREDIT))
                    act.activation(weight_part(0, u, w, n), half(w32[:, n, :], u), ACT.Copy).then_inc(w_high, 1)

            for u in range(UNITS):
                weight_high(u, u, 0)

            def body(st, group, pairs, all_steps, j, first):
                for m in range(2):
                    use = (all_steps + j) * 2 + m
                    h = hid[:, m, :]
                    act.wait_ge(g_done, use + 1)
                    act.wait_ge(inter_split, use + 1)
                    act.activation(h, g_bank[m][:, :], ACT.Square, scale=C2 ** 0.5).then_inc(square_done, 1)
                    act.wait_ge(poly_done, use + 1)
                    act.activation(h, h, ACT.Tanh, scale=C1).then_inc(tanh_done, 1)
                    if m == 0:
                        act.wait_ge(d_done, (all_steps + j) * SUB + 1)
                    act.wait_ge(hid_done, use + (1 + HID_CREDIT))
                    act.activation(inter[0][:, j % 2, m, :], h, ACT.Copy).then_inc(inter_high, 1)
                g, u = j // ST, j % ST
                if u < UNITS:
                    if u == 0:
                        act.wait_ge(d_done, pairs * (2 * ST * SUB) + (g * ST * SUB + D_CREDIT))
                    weight_high(pairs * (2 * UNITS) + ((g + 1) * UNITS + u), u, (g + 1) % 2)

            def tail(st):
                act.wait_ge(var_done, st + 1)
                act.activation(std[:, :], var_eps[:, :], ACT.Sqrt).then_inc(std_done, 1)

            steps(act, tail, body)

        @block.vector
        def _(dve):
            for t in range(ST):
                dve.sem_inc(out_stored[t], OUT_CREDIT)
            dve.sem_inc(u_done, U_CREDIT)
            dve.sem_inc(hid_done, HID_CREDIT)
            dve.sem_inc(inter_split, SPLIT_CREDIT)
            dve.sem_inc(d_added, ADD_CREDIT)
            dve.sem_inc(d_done, D_CREDIT)
            dve.sem_inc(w_made, W_CREDIT)
            dve.sem_inc(w_split, SPLITW_CREDIT)

            def unpack(number, loads, u, parity):
                step = number * 5
                dve.wait_ge(unit_loaded[parity], loads * 48)
                dve.wait_ge(w_made, number * 2 + W_CREDIT)
                raw = codes[:, parity, :]
                dve.tensor_scalar(bits_a[:, :], raw, 0xF0, 12, ALU.bitwise_and,
                                  ALU.logical_shift_left).then_inc(bit_step, 1)
                dve.wait_ge(bit_step, step + 1)
                dve.scalar_tensor_tensor(bits_b[:, :], raw, 0x0F, bits_a[:, :], ALU.bitwise_and,
                                         ALU.bitwise_or).then_inc(bit_step, 1)
                dve.wait_ge(bit_step, step + 2)
                dve.tensor_scalar(bits_a[:, :], bits_b[:, :], 0x00070007, 9, ALU.bitwise_and,
                                  ALU.logical_shift_left).then_inc(bit_step, 1)
                dve.tensor_scalar(bits_b[:, :], bits_b[:, :], 0x00080008, 12, ALU.bitwise_and,
                                  ALU.logical_shift_left).then_inc(bit_step, 1)
                dve.wait_ge(bit_step, step + 4)
                dve.tensor_tensor(bits_a[:, :], bits_a[:, :], bits_b[:, :], ALU.bitwise_or).then_inc(bit_step, 1)
                dve.wait_ge(bit_step, step + 5)
                value = bits_a[:, :].bitcast(F16).rearrange("p (n e) -> p e n", e=2)
                for n in range(2):
                    dve.wait_ge(w_split, number * 2 + (n + 1))
                    dve.scalar_tensor_tensor(w32[:, n, :], value[:, n, :], 2.0 ** 14, scale[:, parity, :],
                                             ALU.mult, ALU.mult).then_inc(w_made, 1)

            for u in range(UNITS):
                unpack(u, (1, 1, 2)[u], u, u % 2)

            def add_down(step, t, q):
                dve.wait_ge(d_done, step * SUB + (q + 1 + D_CREDIT))
                a = acc[:, t * SUB + q, :]
                dve.tensor_tensor(a, a, d_bank[q][:, :], ALU.add).then_inc(d_added, 1)

            def body(st, group, pairs, all_steps, j, first):
                for m in range(2):
                    use = (all_steps + j) * 2 + m
                    h = hid[:, m, :]
                    dve.wait_ge(square_done, use + 1)
                    dve.scalar_tensor_tensor(h, h, 1.0, g_bank[m][:, :], ALU.add, ALU.mult).then_inc(poly_done, 1)
                    for q in (2 * m, 2 * m + 1):
                        if not (first and j < 2):
                            if first and j < 6 and q == 0:
                                dve.wait_ge(acc_loaded[j - 2], st * 16 + 16)
                            add_down(all_steps + (j - 2), (j - 2) % ST, q)
                    dve.wait_ge(tanh_done, use + 1)
                    dve.scalar_tensor_tensor(h, h, 1.0, g_bank[m][:, :], ALU.add, ALU.mult).then_inc(gelu_done, 1)
                    dve.wait_ge(u_done, use + (1 + U_CREDIT))
                    dve.wait_ge(gelu_done, use + 1)
                    dve.scalar_tensor_tensor(h, h, 0.5, u_bank[m][:, :], ALU.mult, ALU.mult).then_inc(hid_done, 1)
                g, u = j // ST, j % ST
                if u < UNITS:
                    unit = (g + 1) * UNITS + u
                    unpack(pairs * (2 * UNITS) + unit, pairs * UNITS + (unit // 2 + 1), u, unit % 2)

            def tail(st):
                for j in (STEPS - 2, STEPS - 1):
                    for q in range(SUB):
                        add_down(st * STEPS + j, j % ST, q)
                n = SUPER // P
                dve.wait_ge(d_added, (st + 1) * (STEPS * SUB) + ADD_CREDIT)
                for a in range(n):
                    dve.bn_stats(stats[:, a, :], acc[:, a, :]).then_inc(stat_done, 1)
                for a in range(n):
                    wait_apart(dve, passed, stat_done, st * n + (a + 1))
                    dve.bn_aggr(mean_var[:, a, :], stats[:, a, :]).then_inc(agg_done, 1)
                dve.wait_ge(agg_done, st * n + n)
                dve.tensor_scalar(var_eps[:, :], mean_var[:, :, 1], EPS, None, ALU.add).then_inc(var_done, 1)
                dve.tensor_scalar(neg_mean[:, :], mean_var[:, :, 0], -1.0, None, ALU.mult)
                dve.wait_ge(std_done, st + 1)
                dve.reciprocal(rstd[:, :], std[:, :]).then_inc(rstd_done, 1)

            steps(dve, tail, body)

        @block.gpsimd
        def _(pool):
            def weight_low(number, u, w):
                for n in range(2):
                    pool.wait_ge(w_high, number * 2 + (n + 1))
                    pool.tensor_tensor(weight_part(1, u, w, n), half(w32[:, n, :], u),
                                       f32(weight_part(0, u, w, n)), ALU.subtract).then_inc(w_split, 1)

            for u in range(UNITS):
                weight_low(u, u, 0)

            def body(st, group, pairs, all_steps, j, first):
                for m in range(2):
                    pool.wait_ge(inter_high, (all_steps + j) * 2 + (m + 1))
                    pool.tensor_tensor(inter[1][:, j % 2, m, :], hid[:, m, :],
                                       f32(inter[0][:, j % 2, m, :]), ALU.subtract).then_inc(inter_split, 1)
                g, u = j // ST, j % ST
                if u < UNITS:
                    weight_low(pairs * (2 * UNITS) + ((g + 1) * UNITS + u), u, (g + 1) % 2)

            def tail(st):
                wait_apart(pool, passed, rstd_done, st + 1)
                for a in range(SUPER // P):
                    pool.tensor_scalar(acc[:, a, :], acc[:, a, :], neg_mean[:, a:a + 1], rstd[:, a:a + 1],
                                       ALU.add, ALU.mult).then_inc(out_made, 1)

            steps(pool, tail, body)


def program(nc, a, out):
    def internal(name, shape):
        return nc.dram_tensor(name, shape, F32, kind="Internal").ap()

    x1_dram = internal("x1_scratch", [TOK, HID])
    x1T_dram = internal("x1T_scratch", [2, HID, TOK])
    qk_dram = internal("qk_scratch", [2, P, 2, SEQ])
    bank = [nc.alloc_psum_tensor(f"bank{i}", [P, 512], F32) for i in range(8)]
    attention_phase(nc, bank, a["xT"], a["x"], a["w_qkvT"], a["w_oT"], a["causal"], a["identity"],
                    x1_dram, x1T_dram, qk_dram)
    feed_forward_phase(nc, bank, x1_dram, x1T_dram, (a["gate"], a["up"], a["down"]),
                       (a["gate_scales"], a["up_scales"], a["down_scales"]), out)


def kernel(L0_attn_hidden_states, L0_attn_w_qkv, L0_attn_w_o, L0_ffn_gate_W_packed, L0_ffn_gate_scales,
           L0_ffn_up_W_packed, L0_ffn_up_scales, L0_ffn_down_W_packed, L0_ffn_down_scales):
    import numpy as np
    import concourse.bacc as bacc
    from concourse.bass_utils import run_bass_kernel_spmd

    def by_input(w):
        w = np.asarray(w)
        return np.ascontiguousarray(w.T.reshape(-1, MLP // GW, P, 2).transpose(0, 1, 3, 2).reshape(-1, MLP))

    x = np.ascontiguousarray(np.asarray(L0_attn_hidden_states).reshape(TOK, HID))
    causal = np.zeros((P, SEQ), np.float32)
    causal[:, SEQ - P:][np.triu_indices(P, 1)] = MASKED
    arrays = {
        "xT": np.ascontiguousarray(x.T),
        "x": x,
        "w_qkvT": np.ascontiguousarray(np.asarray(L0_attn_w_qkv).T),
        "w_oT": np.ascontiguousarray(np.asarray(L0_attn_w_o).T),
        "causal": causal,
        "identity": np.eye(P, dtype=np.float32),
        "gate": by_input(L0_ffn_gate_W_packed),
        "up": by_input(L0_ffn_up_W_packed),
        "down": np.ascontiguousarray(np.asarray(L0_ffn_down_W_packed).T),
        "gate_scales": by_input(L0_ffn_gate_scales),
        "up_scales": by_input(L0_ffn_up_scales),
        "down_scales": np.ascontiguousarray(np.asarray(L0_ffn_down_scales).T),
    }
    nc = bacc.Bacc("TRN2", target_bir_lowering=False, num_devices=1)
    aps = {n: nc.dram_tensor(n, v.shape, mybir.dt.from_np(v.dtype), kind="ExternalInput").ap() for n, v in arrays.items()}
    out = nc.dram_tensor("out", [TOK, HID], F32, kind="ExternalOutput").ap()
    program(nc, aps, out)
    result = run_bass_kernel_spmd(nc, [arrays], core_ids=[0])
    return result.results[0]["out"].reshape(BATCH, SEQ, HID)
```

```python
import concourse.bass as bass
from concourse import mybir

F32 = mybir.dt.float32
F32R = mybir.dt.float32r
I32 = mybir.dt.int32
F16 = mybir.dt.float16
ALU = mybir.AluOpType
ACT = mybir.ActivationFunctionType

P = 128
BATCH, SEQ, HID = 8, 512, 512
HEADS = 16
HD = HID // HEADS
MLP = 4096
EPS = 1e-5
SCALE = float(HD) ** -0.5
KC = HID // P
TT = SEQ // P
GROUPS = HEADS // 4
TOK = BATCH * SEQ
MASKED = -1e30
PCOL = [0, 128, 384, 768]
TCOL = [0, 512, 896, 1280]
PW = 1280
TW = 1408
FULL_RATE = 256
STORED_CREDIT = 16


class Plan:

    def __init__(self, nc):
        self.nc, self.at, self.where = nc, (nc.sbuf_base + 63) // 64 * 64, {}

    def __call__(self, name, shape, dtype, over=None, skip=0):
        size = 4
        for n in shape[1:]:
            size *= n
        offset = self.where[over] + skip if over else self.at
        if not over:
            self.at += (size + 31) // 32 * 32
        self.where[name] = offset
        return self.nc.alloc_sbuf_tensor_at(name, shape, dtype, offset=offset)


def wait_apart(eng, passed, semaphore, value):
    eng.wait_ge(semaphore, value)
    eng.sem_inc(passed, 1)


def f32(ap):
    return ap.bitcast(F32)


def attention_phase(nc, bank, xT_dram, x_dram, wqkvT, woT, tri, ident_dram, x1_dram, x1T_dram, qk_dram):
    plan = Plan(nc)
    w_h = plan("w_h", [P, KC, 3 * HID], F32R)
    w_l = plan("w_l", [P, KC, 3 * HID], F32R)
    wo_h = plan("wo_h", [P, KC, HID], F32R)
    wo_l = plan("wo_l", [P, KC, HID], F32R)
    x_h = plan("x_h", [P, KC, SEQ], F32R)
    x_l = plan("x_l", [P, KC, SEQ], F32R)
    xs = plan("xs", [P, 2, SEQ], F32)
    qk_stage = plan("qk_stage", [P, 2, SEQ], F32)
    q_st = plan("q_st", [P, 2, 4, SEQ], F32R)
    k_st = plan("k_st", [P, 2, 4, SEQ], F32R)
    v_pad = plan("v_pad", [P, TT, HEADS, P], F32R)
    probs = plan("probs", [P, 4, PW], F32)
    w_stage = plan("w_stage", [P, 2, 4 * HID], F32, over="probs")
    pT_h = plan("pT_h", [P, TW], F32R)
    pT_l = plan("pT_l", [P, TW], F32R)
    lo_part = plan("lo_part", [64, SEQ], F32)
    a_sum = plan("a_sum", [P, SEQ], F32)
    a_h = plan("a_h", [P, KC, SEQ], F32R)
    a_l = plan("a_l", [P, KC, SEQ], F32R)
    y = plan("y", [P, TT, HID], F32)
    x1_stage = plan("x1_stage", [P, 2, 2, SEQ], F32)
    mask = plan("mask", [P, SEQ], F32)
    ident = plan("ident", [P, P], F32)
    neg_max = plan("neg_max", [P, 4, TT], F32)
    row_sum = plan("row_sum", [P, 4, TT], F32)
    row_inv = plan("row_inv", [P, 4, TT], F32)
    stats = plan("stats", [P, TT, 6], F32)
    mean_var = plan("mean_var", [P, TT, 2], F32)
    var_eps = plan("var_eps", [P, TT], F32)
    neg_half = plan("neg_half", [P, TT], F32)
    newton = plan("newton", [P, TT], F32)
    rstd = plan("rstd", [P, TT], F32)
    assert plan.at <= nc.sbuf_usable_end, plan.at

    proj_bank, s_bank, t_bank, o_bank = bank[0:2], bank[2:4], bank[4:6], bank[6:8]

    sem = lambda name: nc.alloc_semaphore("a_" + name)
    const_loaded = sem("const_loaded")
    w_loaded = [sem("w_loaded0"), sem("w_loaded1")]
    w_high, w_split = sem("w_high"), sem("w_split")
    zeroed = sem("zeroed")
    x_loaded = [sem("x_loaded0"), sem("x_loaded1")]
    x_high, x_split = sem("x_high"), sem("x_split")
    proj_done, proj_high, proj_free = sem("proj_done"), sem("proj_high"), sem("proj_free")
    qk_written = sem("qk_written")
    stack_loaded = [sem("stack_loaded0"), sem("stack_loaded1")]
    s_done, s_masked = sem("s_done"), sem("s_masked")
    exp_done, inv_done, norm_done = sem("exp_done"), sem("inv_done"), sem("norm_done")
    t_done, t_high, t_free = sem("t_done"), sem("t_high"), sem("t_free")
    pv_done, o_low, o_free = sem("pv_done"), sem("o_low"), sem("o_free")
    a_high, a_split = sem("a_high"), sem("a_split")
    y_loaded, y_stat, y_agg = sem("y_loaded"), sem("y_stat"), sem("y_agg")
    var_done, pow_done, newton_step, x1_done = sem("var_done"), sem("pow_done"), sem("newton_step"), sem("x1_done")
    x1_stored = sem("x1_stored")
    x1T_stored = [sem("x1T_stored0"), sem("x1T_stored1")]
    passed = sem("passed")

    LAG_EXP, LAG_NORM, LAG_T, LAG_PV, LAG_PAIR, LAG_SPLIT = 1, 2, 3, 4, 6, 9

    def head_in(b, s, lag, cur, prev):
        if s >= lag:
            return (b * HEADS + (s - lag), s - lag) if cur and s - lag < HEADS else None
        return (b * HEADS - (lag - s), s - lag + HEADS) if prev else None

    def pair_in(b, s, cur, prev):
        if s % 2:
            return None
        if s >= LAG_PAIR:
            return (b * 8 + (s - LAG_PAIR) // 2, (s - LAG_PAIR) // 2) if cur else None
        return (b * 8 - (LAG_PAIR - s) // 2, 8 - (LAG_PAIR - s) // 2) if prev else None

    def group_in(b, s, cur, prev):
        if s % 4 != 1:
            return None
        if s >= LAG_SPLIT:
            return (b * GROUPS + (s - LAG_SPLIT) // 4, (s - LAG_SPLIT) // 4) if cur else None
        return (b * GROUPS - (LAG_SPLIT - s) // 4, GROUPS - (LAG_SPLIT - s) // 4) if prev else None

    OUT_SLOT = 6
    NEXT_SLOT = OUT_SLOT + TT

    def projections(cur, prev, nxt):
        plan_ = {}
        if cur:
            plan_ = {0: [("q", 2)], 1: [("k", 2)], 2: [("q", 3)], 3: [("k", 3)],
                     4: [("v_second", 0), ("v_second", 1)], 5: [("v_second", 2), ("v_second", 3)]}
        if prev:
            for t in range(TT):
                plan_[OUT_SLOT + t] = [("out", t)]
        if nxt:
            plan_.update({10: [("q", 0)], 11: [("k", 0)], 12: [("q", 1)], 13: [("k", 1)],
                          14: [("v_first", 0), ("v_first", 1)], 15: [("v_first", 2), ("v_first", 3)]})
        placed, use, high = {}, 0, 0
        for s in sorted(plan_):
            for kind, n in plan_[s]:
                placed.setdefault(s, []).append((kind, n, use, high))
                use += 1
                high += kind != "out"
        return placed

    def split_after(todo, s, k):
        return [work for i, work in enumerate(todo.get(s, ())) if (i + 1) * TT // len(todo[s]) == k + 1]

    def uses_before(slot, cur, prev, nxt):
        return sum(len(v) for s, v in projections(cur, prev, nxt).items() if s < slot)

    PRE = 8
    def use_base(b, cur, prev):
        if not prev:
            return PRE
        return b * 20 + 4 if cur else BATCH * 20 + 4 - 8

    def high_base(b):
        return b * 16 + PRE

    NORM_SLOT = 10
    NORM_STEPS = [(10, 2), (10, 3), (11, 1), (11, 2)]
    X1T_SLOTS = {11: (0, 1), 14: (2, 3)}

    def t_use(b, s, k, cur, prev):
        if not prev:
            return (s - LAG_T) * TT + k
        return b * 68 - 16 + s * TT + k + (4 if s > 14 else 2 if s > 11 else 0)

    def x1T_use(b, t, cur):
        return b * 68 - 16 + ((48, 49, 62, 63)[t] if cur else 12 + t)

    CREDIT = 2

    def batches(eng, body):
        body(0, True, False, True)
        with eng.Fori(1, BATCH - 1) as b:
            body(b, True, True, True)
        body(BATCH - 1, True, True, False)
        body(BATCH, False, True, False)

    SLOTS = HEADS
    block = nc.Block()
    with block as block:

        @block.sync
        def _(sp):
            def load_x(b, c):
                if c >= 2:
                    sp.wait_ge(x_split, b * KC + (c - 1))
                sp.dma_start(xs[:, c % 2, :], xT_dram[c * P:(c + 1) * P, bass.ts(b, SEQ)]).then_inc(x_loaded[c % 2], 16)

            def write_qk(use, which, c):
                sp.wait_ge(proj_free, use + 3)
                sp.dma_start(qk_dram[c % 2, which], qk_stage[:]).then_inc(qk_written, 16)

            def read_first_stack(c, written):
                wait_apart(sp, passed, qk_written, written * 16)
                read_stack(0, c)

            def read_stack(which, c):
                for j in range(4):
                    part = j % 2 if which == 0 else j // 2
                    src = qk_dram[c % 2, which][:, part, :].rearrange("(g p) t -> p g t", g=4)
                    sp.dma_start(f32((q_st, k_st)[which][32 * j:32 * j + 32, c % 2, :, :]),
                                 src).then_inc(stack_loaded[c % 2], 16)

            load_x(0, 0)
            load_x(0, 1)
            for c in range(KC):
                if c >= 2:
                    sp.wait_ge(w_split, 2 * (c - 1))
                sp.dma_start(w_stage[:, c % 2, 0:3 * HID], wqkvT[c * P:(c + 1) * P, :]).then_inc(w_loaded[c % 2], 16)
                sp.dma_start(w_stage[:, c % 2, 3 * HID:], woT[c * P:(c + 1) * P, :]).then_inc(w_loaded[c % 2], 16)
            load_x(0, 2)
            load_x(0, 3)
            sp.dma_start(mask[:], tri).then_inc(const_loaded, 16)
            sp.dma_start(ident[:], ident_dram).then_inc(const_loaded, 16)
            for i, (kind, c) in enumerate((("q", 0), ("k", 0), ("q", 1), ("k", 1))):
                write_qk(2 * i, "qk".index(kind), c)
                if kind == "k":
                    read_first_stack(c, 2 * c + 2)
                    read_stack(1, c)

            def body(b, cur, prev, nxt):
                base, todo = use_base(b, cur, prev), projections(cur, prev, nxt)
                for s in range(SLOTS):
                    for kind, c, use, _ in todo.get(s, []):
                        if kind in "qk":
                            if kind == "q":
                                wait_apart(sp, passed, stack_loaded[c % 2], b * 256 + (128 if c >= 2 else 256))
                            write_qk(base + use, "qk".index(kind), c)
                    if OUT_SLOT <= s + 1 < NEXT_SLOT and nxt:
                        for c in (0, 1) if s + 1 == OUT_SLOT else (s + 2 - OUT_SLOT,) if s + 2 < NEXT_SLOT else ():
                            load_x(b + 1, c)
                    for t in X1T_SLOTS.get(s - 1, ()):
                        if prev:
                            wait_apart(sp, passed, t_free, x1T_use(b, t, cur) + 3)
                            tok = (b - 1) * SEQ + t * P
                            for part in range(2):
                                sp.dma_start(
                                    x1T_dram[part].rearrange("(c p) t -> p c t", p=P)[:, :, bass.ds(tok, P)],
                                    x1_stage[:, t % 2, part, :].rearrange("p (c t) -> p c t", c=KC)).then_inc(x1T_stored[t % 2], 16)
                    if s % 4 == 3 and (cur if s < 8 else nxt):
                        wait_apart(sp, passed, s_done, (b * HEADS + s + 1) * TT)
                        read_first_stack((s // 4 + 2) % 4, b * 8 + (6 + s // 4 * 2))
                    if s % 4 == 1 and (nxt if s == 13 else cur and (s > 1 or prev)):
                        read_stack(1, (s // 4 + 1) % 4)
                    if s == 14 and prev:
                        wait_apart(sp, passed, x1_done, b * TT)
                        sp.dma_start(x1_dram[bass.ts(b - 1, SEQ), :].rearrange("(t p) h -> p t h", p=P),
                                     y[:]).then_inc(x1_stored, 16)
                    if s == 4 and prev:
                        wait_apart(sp, passed, t_done, x1T_use(b, 3, True) - 67)
                        wait_apart(sp, passed, x1_stored, b * 16)
                        sp.dma_start(y[:], x_dram[bass.ts(b - 1, SEQ), :].rearrange("(t p) h -> p t h", p=P)).then_inc(y_loaded, 16)

            batches(sp, body)
            sp.wait_ge(x1_stored, BATCH * 16 + STORED_CREDIT)
            for stored in x1T_stored:
                sp.wait_ge(stored, BATCH * TT // 2 * 32 + STORED_CREDIT)

        @block.tensor
        def _(pe):
            def project(use, parity, kind, n, c):
                if c == 0:
                    pe.wait_ge(proj_free, use + 1)
                if kind in "qk":
                    out, left, right = proj_bank[parity][:, :], (w_h, w_l), (x_h, x_l)
                    cols = slice(0, SEQ)
                    first = "qk".index(kind) * HID + n * P
                    rows = slice(first, first + P)
                elif kind == "out":
                    out, left, right = proj_bank[parity][:, :], (a_h, a_l), (wo_h, wo_l)
                    rows, cols = slice(n * P, (n + 1) * P), slice(0, HID)
                else:
                    out, left, right = proj_bank[parity][:, 0:HID // 2], (x_h, x_l), (w_h, w_l)
                    first = 2 * HID + (HID // 2 if kind == "v_second" else 0)
                    rows, cols = slice(n * P, (n + 1) * P), slice(first, first + HID // 2)
                passes = ((0, 0), (0, 1), (1, 0))
                for i, (l, r) in enumerate(passes):
                    last = pe.matmul(out, left[l][:, c, rows], right[r][:, c, cols],
                                     start=(c == 0 and i == 0), stop=(c == KC - 1 and i == 2))
                if c == KC - 1:
                    last.then_inc(proj_done, 1)

            def scores(b, s, k):
                use = (b * HEADS + s) * TT + k
                pe.wait_ge(s_masked, use + 1)
                g, st = s % 4, s // 4 % 2
                n = max(P * (k + 1), FULL_RATE)
                pe.matmul(s_bank[k % 2][:, 0:n], q_st[:, st, g, k * P:(k + 1) * P], k_st[:, st, g, 0:n],
                          start=True, stop=True).then_inc(s_done, 1)

            def transpose_probs(use, count, h, k):
                if k == 0:
                    pe.wait_ge(norm_done, count * TT + TT)
                pe.wait_ge(t_free, use + 1)
                for i in range(k, TT):
                    last = pe.transpose(t_bank[k % 2][:, (i - k) * P:(i - k + 1) * P],
                                        probs[:, h % 4, PCOL[i] + k * P:PCOL[i] + (k + 1) * P], ident[:])
                last.then_inc(t_done, 1)

            def values(use, h, k):
                pe.wait_ge(t_free, use + 3)
                n = max(SEQ - k * P, FULL_RATE)
                out = o_bank[h // 2 % 2][:, SEQ - n:SEQ]
                col = TCOL[k] + SEQ - k * P - n
                pe.matmul(out, v_pad[:, k, h, :], pT_h[:, col:col + n],
                          start=(h % 2 == 0 and k == 0), stop=False, skip_group_check=True)
                pe.matmul(out, v_pad[:, k, h, :], pT_l[:, col:col + n],
                          start=False, stop=(h % 2 == 1 and k == TT - 1), skip_group_check=True).then_inc(pv_done, 1)

            def transpose_x1(use, t):
                pe.wait_ge(t_free, use + 1)
                for c in range(KC):
                    first = c // 2 * 256 + c % 2
                    last = pe.transpose(t_bank[t % 2][:, c * P:(c + 1) * P], y[:, t, first:first + 255:2], ident[:])
                last.then_inc(t_done, 1)

            pe.wait_ge(w_split, 2 * KC)
            pe.wait_ge(x_split, KC)
            for i, (kind, c) in enumerate((("q", 0), ("k", 0), ("q", 1), ("k", 1))):
                for j in range(KC):
                    project(2 * i, 0, kind, c, j)
                for j in range(KC):
                    project(2 * i + 1, 1, "v_first", i, j)
            pe.wait_ge(const_loaded, 32)

            def body(b, cur, prev, nxt):
                base, todo = use_base(b, cur, prev), projections(cur, prev, nxt)
                for s in range(SLOTS):
                    if cur and s % 4 == 0:
                        c = s // 4
                        pe.wait_ge(stack_loaded[c % 2], b * 256 + (c // 2 + 1) * 128)
                    if cur and s == 4:
                        pe.wait_ge(proj_free, base + 2)
                    if cur and s == 12:
                        pe.wait_ge(proj_free, base + uses_before(OUT_SLOT, cur, prev, nxt) + 2)
                    pieces = [(kind, n, use, c) for kind, n, use, _ in todo.get(s, []) for c in range(KC)]
                    t_head, v_head = head_in(b, s, LAG_T, cur, prev), head_in(b, s, LAG_PV, cur, prev)
                    for k in range(TT):
                        if cur:
                            scores(b, s, k)
                        for kind, n, use, c in pieces[k * len(pieces) // TT:(k + 1) * len(pieces) // TT]:
                            if s == OUT_SLOT:
                                pe.wait_ge(a_split, b * GROUPS - (GROUPS - 1 - c))
                            if s == NEXT_SLOT:
                                pe.wait_ge(x_split, b * KC + (KC + 1 + c))
                            project(base + use, use % 2, kind, n, c)
                        if v_head:
                            if v_head[1] % 2 == 0 and k == 0:
                                if s >= LAG_PV:
                                    pe.wait_ge(o_free, b * 8 + ((s - LAG_PV) // 2 + 1))
                                else:
                                    pe.wait_ge(o_free, b * 8 - ((LAG_PV - s) // 2 - 1))
                            use = (t_use(b, s - 1, k, cur, prev) if s else
                                   t_use(b - 1, SLOTS - 1, k, True, not isinstance(b, int) or b > 1))
                            values(use, v_head[1], k)
                        if t_head:
                            transpose_probs(t_use(b, s, k, cur, prev), *t_head, k)
                    for t in X1T_SLOTS.get(s, ()):
                        if prev:
                            pe.wait_ge(x1_done, b * TT - (TT - 1 - t))
                            transpose_x1(x1T_use(b, t, cur), t)

            batches(pe, body)

        @block.scalar
        def _(act):
            def copy(out, in_):
                return act.activation(out, in_, ACT.Copy)

            def x_part(b, c):
                act.wait_ge(x_loaded[c % 2], b * 32 + (c // 2 * 16 + 16))
                copy(x_h[:, c, :], xs[:, c % 2, :]).then_inc(x_high, 1)

            def project_high(nth, parity, kind, n, sent):
                act.wait_ge(proj_done, nth + 1)
                if kind in "qk":
                    act.wait_ge(qk_written, sent * 16)
                    copy(qk_stage[:, 0, :].bitcast(F32R), proj_bank[parity][:, :]).then_inc(proj_high, 1)
                else:
                    first = HEADS // 2 if kind == "v_second" else 0
                    v = proj_bank[parity][:, 0:HID // 2].rearrange("p (g e d) -> p e g d", e=2, d=HD)
                    dst = v_pad[:, n, first:first + HEADS // 2, :].rearrange("p (g e) n -> p e g n", e=2)
                    copy(dst[:, 0, :, 0:HD], v[:, 0, :, :])
                    copy(dst[:, 1, :, HD:2 * HD], v[:, 1, :, :]).then_inc(proj_high, 1)

            x_part(0, 0)
            x_part(0, 1)
            for c in range(KC):
                act.wait_ge(w_loaded[c % 2], 32 * (c // 2 + 1))
                copy(w_h[:, c, :], w_stage[:, c % 2, 0:3 * HID]).then_inc(w_high, 1)
                copy(wo_h[:, c, :], w_stage[:, c % 2, 3 * HID:]).then_inc(w_high, 1)
            x_part(0, 2)
            x_part(0, 3)
            act.wait_ge(zeroed, 1)
            for i, (kind, c) in enumerate((("q", 0), ("k", 0), ("q", 1), ("k", 1))):
                project_high(2 * i, 0, kind, c, i)
                project_high(2 * i + 1, 1, "v_first", i, None)

            def body(b, cur, prev, nxt):
                base, todo = use_base(b, cur, prev), projections(cur, prev, nxt)
                sent = b * 8 + 4
                for s in range(SLOTS):
                    e_head, t_head = head_in(b, s, LAG_EXP, cur, prev), head_in(b, s, LAG_T, cur, prev)
                    v_head, pair = head_in(b, s, LAG_PV, cur, prev), pair_in(b, s, cur, prev)
                    for k in range(TT):
                        if e_head:
                            count, h = e_head
                            n = P * (k + 1)
                            act.wait_ge(s_masked, count * TT + (k + 3))
                            p = probs[:, h % 4, PCOL[k]:PCOL[k] + n]
                            act.activation(p, p, ACT.Exp, bias=neg_max[:, h % 4, k:k + 1], scale=-1.0,
                                           accum_out=row_sum[:, h % 4, k:k + 1]).then_inc(exp_done, 1)
                        if t_head:
                            n = SEQ - k * P
                            act.wait_ge(t_done, t_use(b, s, k, cur, prev) + 1)
                            if v_head:
                                act.wait_ge(pv_done, v_head[0] * TT + (k + 1))
                            copy(pT_h[:, TCOL[k]:TCOL[k] + n], t_bank[k % 2][:, 0:n]).then_inc(t_high, 1)
                        if k == 0 and pair:
                            count, p = pair
                            act.wait_ge(pv_done, count * (2 * TT) + 2 * TT)
                            act.wait_ge(o_free, count + 2)
                            copy(lo_part[:, :], o_bank[p % 2][64:P, :]).then_inc(o_low, 1)
                        if k == 1 and OUT_SLOT <= s < NEXT_SLOT and nxt:
                            if s == OUT_SLOT:
                                act.wait_ge(proj_done, base + uses_before(OUT_SLOT, cur, prev, nxt))
                            x_part(b + 1, s - OUT_SLOT)
                        for kind, n, use, _ in split_after(todo, s, k):
                            if kind == "v_second" and n == 0 and prev:
                                act.wait_ge(pv_done, b * (HEADS * TT))
                            if kind == "v_first" and n == 0:
                                act.wait_ge(pv_done, (b * HEADS + 8) * TT)
                            if kind != "out":
                                project_high(base + use, use % 2, kind, n, sent)
                                sent = sent + (kind in "qk")
                    for t in X1T_SLOTS.get(s, ()):
                        if prev:
                            act.wait_ge(t_done, x1T_use(b, t, cur) + 1)
                            act.wait_ge(x1T_stored[t % 2], b * 64 - (64 - t // 2 * 32 - STORED_CREDIT))
                            copy(x1_stage[:, t % 2, 0, :].bitcast(F32R), t_bank[t % 2][:, :]).then_inc(t_high, 1)
                    group = group_in(b, s, cur, prev)
                    if group:
                        count, c = group
                        act.wait_ge(o_free, count * 2 + 4)
                        if c == 0 and prev:
                            act.wait_ge(proj_done, base + uses_before(NEXT_SLOT, cur, prev, nxt))
                        copy(a_h[:, c, :], a_sum[:, :]).then_inc(a_high, 1)

            batches(act, body)

        @block.vector
        def _(dve):
            def low(out, whole, high):
                return dve.tensor_tensor(out, whole, high, ALU.subtract)

            dve.sem_inc(proj_free, CREDIT)
            dve.sem_inc(t_free, CREDIT)
            dve.sem_inc(s_masked, CREDIT)
            dve.sem_inc(o_free, CREDIT)
            for n in (x1_stored, *x1T_stored):
                dve.sem_inc(n, STORED_CREDIT)
            dve.memset(neg_half[:], -0.5)

            def x_part(b, c):
                dve.wait_ge(x_high, b * KC + (c + 1))
                low(x_l[:, c, :], xs[:, c % 2, :], f32(x_h[:, c, :])).then_inc(x_split, 1)

            x_part(0, 0)
            x_part(0, 1)
            for c in range(KC):
                dve.wait_ge(w_high, 2 * c + 1)
                low(w_l[:, c, :], w_stage[:, c % 2, 0:3 * HID], f32(w_h[:, c, :])).then_inc(w_split, 1)
                dve.wait_ge(w_high, 2 * c + 2)
                low(wo_l[:, c, :], w_stage[:, c % 2, 3 * HID:], f32(wo_h[:, c, :])).then_inc(w_split, 1)
            x_part(0, 2)
            x_part(0, 3)

            def project_low(high, parity, kind, n):
                dve.wait_ge(proj_high, high + 1)
                if kind in "qk":
                    low(qk_stage[:, 1, :].bitcast(F32R), proj_bank[parity][:, :], qk_stage[:, 0, :]).then_inc(proj_free, 1)
                else:
                    first = HEADS // 2 if kind == "v_second" else 0
                    v = proj_bank[parity][:, 0:HID // 2].rearrange("p (g e d) -> p e g d", e=2, d=HD)
                    dst = v_pad[:, n, first:first + HEADS // 2, :].rearrange("p (g e) n -> p e g n", e=2)
                    low(dst[:, 0, :, 64:64 + HD], v[:, 0, :, :], f32(dst[:, 0, :, 0:HD]))
                    low(dst[:, 1, :, 64 + HD:P], v[:, 1, :, :], f32(dst[:, 1, :, HD:2 * HD])).then_inc(proj_free, 1)

            for i, (kind, c) in enumerate((("q", 0), ("k", 0), ("q", 1), ("k", 1))):
                project_low(2 * i, 0, kind, c)
                project_low(2 * i + 1, 1, "v_first", i)
            dve.wait_ge(const_loaded, 32)

            def add_residual(b, use, parity, t):
                if t == 0:
                    dve.wait_ge(y_loaded, b * 16)
                dve.wait_ge(proj_done, use + 1)
                dve.tensor_tensor(y[:, t, :], proj_bank[parity][:, :], y[:, t, :], ALU.add).then_inc(proj_free, 1)
                dve.wait_ge(proj_free, use + 3)
                dve.bn_stats(stats[:, t, :], y[:, t, :]).then_inc(y_stat, 1)
                wait_apart(dve, passed, y_stat, b * TT - (TT - 1 - t))
                dve.bn_aggr(mean_var[:, t, :], stats[:, t, :]).then_inc(y_agg, 1)

            def body(b, cur, prev, nxt):
                base, todo = use_base(b, cur, prev), projections(cur, prev, nxt)
                for s in range(SLOTS):
                    n_head, t_head = head_in(b, s, LAG_NORM, cur, prev), head_in(b, s, LAG_T, cur, prev)
                    pair, group = pair_in(b, s, cur, prev), group_in(b, s, cur, prev)
                    if n_head:
                        count, h = n_head
                        dve.wait_ge(exp_done, count * TT + TT)
                        dve.reciprocal(row_inv[:, h % 4, :], row_sum[:, h % 4, :]).then_inc(inv_done, 1)
                    for k in range(TT):
                        if cur:
                            n = P * (k + 1)
                            if k == 0 and (s >= 4 or prev):
                                before = (t_use(b, s - 1, TT, cur, prev) if s else
                                          t_use(b - 1, SLOTS - 1, TT, True, not isinstance(b, int) or b > 1))
                                dve.wait_ge(t_done, before)
                            wait_apart(dve, passed, s_done, (b * HEADS + s) * TT + (k + 1))
                            dve.tensor_tensor_reduce(
                                probs[:, s % 4, PCOL[k]:PCOL[k] + n], s_bank[k % 2][:, 0:n], mask[:, SEQ - n:SEQ],
                                -SCALE, 3.0e38, ALU.add, ALU.min, neg_max[:, s % 4, k:k + 1]).then_inc(s_masked, 1)
                        if t_head:
                            n = SEQ - k * P
                            dve.wait_ge(t_high, t_use(b, s, k, cur, prev) + 1)
                            low(pT_l[:, TCOL[k]:TCOL[k] + n], t_bank[k % 2][:, 0:n],
                                f32(pT_h[:, TCOL[k]:TCOL[k] + n])).then_inc(t_free, 1)
                        if k == 0 and pair:
                            count, p = pair
                            dve.wait_ge(o_low, count + 1)
                            if p % 2 == 0 and (p or prev):
                                dve.wait_ge(a_split, (b * GROUPS + p // 2) if s >= LAG_PAIR else (b * GROUPS - (GROUPS - p // 2)))
                            r = 64 * (p % 2)
                            dve.tensor_tensor(a_sum[r:r + 64, :], o_bank[p % 2][0:64, :], lo_part[:, :],
                                              ALU.add).then_inc(o_free, 1)
                        for kind, n, use, high in split_after(todo, s, k):
                            if kind == "out":
                                add_residual(b, base + use, use % 2, n)
                            else:
                                project_low(high_base(b) + high, use % 2, kind, n)
                        if s == NORM_SLOT and k == 1 and prev:
                            dve.wait_ge(pow_done, b)
                            dve.tensor_tensor(newton[:, :], var_eps[:, :], rstd[:, :], ALU.mult).then_inc(newton_step, 1)
                            dve.wait_ge(newton_step, b * 3 - 2)
                            dve.scalar_tensor_tensor(newton[:, :], newton[:, :], -0.5, rstd[:, :], ALU.mult,
                                                     ALU.mult).then_inc(newton_step, 1)
                            dve.wait_ge(newton_step, b * 3 - 1)
                            dve.scalar_tensor_tensor(rstd[:, :], newton[:, :], 1.5, rstd[:, :], ALU.add,
                                                     ALU.mult).then_inc(newton_step, 1)
                        if (s, k) in NORM_STEPS and prev:
                            t = NORM_STEPS.index((s, k))
                            dve.wait_ge(newton_step, b * 3)
                            dve.tensor_scalar(y[:, t, :], y[:, t, :], mean_var[:, t, 0:1], rstd[:, t:t + 1],
                                              ALU.subtract, ALU.mult).then_inc(x1_done, 1)
                    for t in X1T_SLOTS.get(s, ()):
                        if prev:
                            dve.wait_ge(t_high, x1T_use(b, t, cur) + 1)
                            low(x1_stage[:, t % 2, 1, :].bitcast(F32R), t_bank[t % 2][:, :],
                                x1_stage[:, t % 2, 0, :]).then_inc(t_free, 1)
                    if group:
                        count, c = group
                        dve.wait_ge(a_high, count + 1)
                        low(a_l[:, c, :], a_sum[:, :], f32(a_h[:, c, :])).then_inc(a_split, 1)
                    if s == NEXT_SLOT - 1 and prev:
                        dve.wait_ge(y_agg, b * TT)
                        dve.tensor_scalar(var_eps[:, :], mean_var[:, :, 1], EPS, None, ALU.add).then_inc(var_done, 1)

            batches(dve, body)

        @block.gpsimd
        def _(pool):
            pool.memset(f32(pT_h[:]), 0.0)
            pool.memset(f32(pT_l[:]), 0.0)
            pool.memset(f32(v_pad[:]), 0.0).then_inc(zeroed, 1)

            def body(b, cur, prev, nxt):
                for s in range(SLOTS):
                    head = head_in(b, s, LAG_NORM, cur, prev)
                    if s == NORM_SLOT and prev:
                        pool.wait_ge(var_done, b)
                        pool.tensor_tensor(rstd[:, :], var_eps[:, :], neg_half[:, :], ALU.pow).then_inc(pow_done, 1)
                    if head:
                        count, h = head
                        wait_apart(pool, passed, inv_done, count + 1)
                        for k in range(TT):
                            p = probs[:, h % 4, PCOL[k]:PCOL[k] + P * (k + 1)]
                            pool.tensor_scalar(p, p, row_inv[:, h % 4, k:k + 1], 1.0, ALU.mult,
                                               ALU.mult).then_inc(norm_done, 1)
                    if OUT_SLOT <= s < NEXT_SLOT and nxt:
                        c = s - OUT_SLOT
                        pool.wait_ge(x_high, (b + 1) * KC + (c + 1))
                        pool.tensor_tensor(x_l[:, c, :], xs[:, c % 2, :], f32(x_h[:, c, :]),
                                           ALU.subtract).then_inc(x_split, 1)

            batches(pool, body)


TILE = 512
SUPER = 2048
NS = TOK // SUPER
ST = SUPER // TILE
SUB = TILE // P
GW = 256
NG = MLP // GW
STEPS = NG * ST
UNITS = 3
BLOCK = 32
C1, C2 = 0.7978845608028654, 0.044715


def feed_forward_phase(nc, bank, x1_dram, x1T_dram, packed, scales, out_dram):
    plan = Plan(nc)
    x_h = plan("bx_h", [P, KC, SUPER], F32R)
    x_l = plan("bx_l", [P, KC, SUPER], F32R)
    acc = plan("acc", [P, SUPER // P, HID], F32)
    wg = [plan(f"wg_{n}", [P, 2, KC, GW], F32R) for n in "hl"]
    wu = [plan(f"wu_{n}", [P, 2, KC, GW], F32R) for n in "hl"]
    wd = [plan(f"wd_{n}", [P, 2, 2, HID], F32R) for n in "hl"]
    inter = [plan(f"inter_{n}", [P, 2, 2, TILE], F32R) for n in "hl"]
    hid = plan("hid", [P, 2, TILE], F32)
    codes = plan("codes", [P, 2, 512], I32)
    scale = plan("scale", [P, 2, 512], F32)
    bits_a = plan("bits_a", [P, 512], I32)
    bits_b = plan("bits_b", [P, 512], I32)
    w32 = plan("w32", [P, 2, 512], F32)
    stats = plan("bstats", [P, SUPER // P, 6], F32)
    mean_var = plan("bmean_var", [P, SUPER // P, 2], F32)
    var_eps = plan("bvar_eps", [P, SUPER // P], F32)
    std = plan("bstd", [P, SUPER // P], F32)
    rstd = plan("brstd", [P, SUPER // P], F32)
    neg_mean = plan("neg_mean", [P, SUPER // P], F32)
    assert plan.at <= nc.sbuf_usable_end, plan.at

    g_bank, u_bank, d_bank = bank[0:2], bank[2:4], bank[4:8]

    sem = lambda name: nc.alloc_semaphore("b_" + name)
    x_loaded = [sem(f"x_loaded{t}") for t in range(ST)]
    acc_loaded = [sem(f"acc_loaded{t}") for t in range(ST)]
    unit_loaded = [sem("unit_loaded0"), sem("unit_loaded1")]
    bit_step = sem("bit_step")
    w_made, w_high, w_split = sem("w_made"), sem("w_high"), sem("w_split")
    g_done, u_done = sem("g_done"), sem("u_done")
    square_done, poly_done, tanh_done = sem("square_done"), sem("poly_done"), sem("tanh_done")
    gelu_done, hid_done = sem("gelu_done"), sem("hid_done")
    inter_high, inter_split = sem("inter_high"), sem("inter_split")
    d_done, d_added = sem("d_done"), sem("d_added")
    stat_done, agg_done = sem("stat_done"), sem("agg_done")
    var_done, std_done, rstd_done = sem("var_done"), sem("std_done"), sem("rstd_done")
    out_made = sem("out_made")
    passed = sem("passed")
    out_stored = [sem(f"out_stored{t}") for t in range(ST)]

    U_CREDIT = 8
    HID_CREDIT = 2
    SPLIT_CREDIT = 2
    ADD_CREDIT = 4
    OUT_CREDIT = 16
    D_CREDIT = 5
    W_CREDIT = 4
    SPLITW_CREDIT = 2
    U2 = 2 * UNITS

    def steps(eng, tail, body):
        with eng.Fori(0, NS) as st:
            for j in range(8):
                body(st, 0, st * (NG // 2), st * STEPS, j, True)
            with eng.Fori(1, NG // 2) as it:
                for j in range(8):
                    body(st, it * 2, st * (NG // 2) + it, st * STEPS + it * 8, j, False)
            tail(st)

    def weight_part(part, u, w, n):
        if u == 2:
            return wd[part][:, w, n, :]
        return (wg, wu)[u][part][:, w, n:KC:2, :]

    def half(ap, u):
        return ap if u == 2 else ap.rearrange("p (c n) -> p c n", c=2)

    block = nc.Block()
    with block as block:

        @block.sync
        def _(sp):
            def load_x(st, t):
                sp.wait_ge(u_done, st * (2 * STEPS) + (2 * t + 2))
                for part, dst in enumerate((x_h, x_l)):
                    src = x1T_dram[part].rearrange("(c p) t -> p c t", p=P)[:, :, bass.ds(st * SUPER + t * TILE, TILE)]
                    sp.dma_start(f32(dst[:, :, t * TILE:(t + 1) * TILE]), src).then_inc(x_loaded[t], 16)

            def load_acc(st, t):
                sp.wait_ge(out_stored[t], st * 16 + OUT_CREDIT)
                src = x1_dram[bass.ds(st * SUPER + t * TILE, TILE), :].rearrange("(a p) h -> p a h", p=P)
                sp.dma_start(acc[:, t * SUB:(t + 1) * SUB, :], src).then_inc(acc_loaded[t], 16)

            def load_unit(number, group, u, parity):
                sp.wait_ge(w_made, number * 2 + 2)
                loaded = unit_loaded[parity]
                if u < 2:
                    cols = bass.ts(group, GW)
                    sp.dma_start(half(codes[:, parity, :], u),
                                 packed[u][:, cols].rearrange("(c p) n -> p c n", p=P)).then_inc(loaded, 16)
                    for c in range(2):
                        src = scales[u][c * 8:(c + 1) * 8, cols].unsqueeze(1).broadcast_to([8, 16, GW])
                        sp.dma_start(scale[:, parity, c * GW:(c + 1) * GW], src).then_inc(loaded, 16)
                else:
                    sp.dma_start(codes[:, parity, :], packed[2][bass.ts(group, P), :]).then_inc(loaded, 16)
                    src = scales[2][bass.ts(group, 8), :].unsqueeze(1).broadcast_to([8, 16, HID])
                    sp.dma_start(scale[:, parity, :], src).then_inc(loaded, 32)

            for u in range(UNITS):
                load_unit(u, 0, u, u % 2)

            def body(st, group, pairs, all_steps, j, first):
                if first and j == 0:
                    for t in range(ST):
                        load_x(st, t)
                        load_acc(st, t)
                g, u = j // ST, j % ST
                if u < UNITS:
                    load_unit(pairs * (2 * UNITS) + ((g + 1) * UNITS + u), (group + (g + 1)) % NG, u, (g + 1 + u) % 2)

            def tail(st):
                for t in range(ST):
                    sp.wait_ge(out_made, st * (SUPER // P) + (t + 1) * SUB)
                    dst = out_dram[bass.ds(st * SUPER + t * TILE, TILE), :].rearrange("(a p) h -> p a h", p=P)
                    sp.dma_start(dst, acc[:, t * SUB:(t + 1) * SUB, :]).then_inc(out_stored[t], 16)

            steps(sp, tail, body)
            for t in range(ST):
                sp.wait_ge(out_stored[t], NS * 16 + OUT_CREDIT)

        @block.tensor
        def _(pe):
            def three(out, a, b, c, count, at, bt):
                pe.matmul(out, at(a[0]), bt(b[0]), start=(c == 0), stop=False)
                pe.matmul(out, at(a[0]), bt(b[1]), start=False, stop=False)
                return pe.matmul(out, at(a[1]), bt(b[0]), start=False, stop=(c == count - 1))

            def gate_up(step, w, t):
                for m in range(2):
                    pe.wait_ge(hid_done, step * 2 + (m + 1))
                    for weights, out, done in ((wg, g_bank[m], g_done), (wu, u_bank[m], u_done)):
                        for c in range(KC):
                            last = three(out[:, :], weights, (x_h, x_l), c, KC,
                                         lambda x: x[:, w, c, m * P:(m + 1) * P],
                                         lambda x: x[:, c, t * TILE:(t + 1) * TILE])
                        last.then_inc(done, 1)

            def down(step, w, parity):
                pe.wait_ge(inter_split, step * 2 + (2 + SPLIT_CREDIT))
                for q in range(SUB):
                    pe.wait_ge(d_added, step * SUB + (q + 1))
                    for m in range(2):
                        last = three(d_bank[q][:, :], inter, wd, m, 2,
                                     lambda x: x[:, parity, m, q * P:(q + 1) * P],
                                     lambda x: x[:, w, m, :])
                    last.then_inc(d_done, 1)

            def body(st, group, pairs, all_steps, j, first):
                g, t = j // ST, j % ST
                if first and g == 0:
                    pe.wait_ge(x_loaded[t], st * 32 + 32)
                if t == 0:
                    pe.wait_ge(w_split, pairs * (2 * U2) + (g * U2 + 4 + SPLITW_CREDIT))
                gate_up(all_steps + j, g, t)
                if not (first and j == 0):
                    if t == 1:
                        pe.wait_ge(w_split, pairs * (2 * U2) + (g * U2 + 6 + SPLITW_CREDIT))
                    down(all_steps + (j - 1), (j - 1) // ST % 2, (j - 1) % 2)

            def tail(st):
                down(st * STEPS + (STEPS - 1), 1, 1)

            steps(pe, tail, body)

        @block.scalar
        def _(act):
            def weight_high(number, u, w):
                for n in range(2):
                    act.wait_ge(w_made, number * 2 + (n + 1 + W_CREDIT))
                    act.activation(weight_part(0, u, w, n), half(w32[:, n, :], u), ACT.Copy).then_inc(w_high, 1)

            for u in range(UNITS):
                weight_high(u, u, 0)

            def body(st, group, pairs, all_steps, j, first):
                for m in range(2):
                    use = (all_steps + j) * 2 + m
                    h = hid[:, m, :]
                    act.wait_ge(g_done, use + 1)
                    act.wait_ge(inter_split, use + 1)
                    act.activation(h, g_bank[m][:, :], ACT.Square, scale=C2 ** 0.5).then_inc(square_done, 1)
                    act.wait_ge(poly_done, use + 1)
                    act.activation(h, h, ACT.Tanh, scale=C1).then_inc(tanh_done, 1)
                    if m == 0:
                        act.wait_ge(d_done, (all_steps + j) * SUB + 1)
                    act.wait_ge(hid_done, use + (1 + HID_CREDIT))
                    act.activation(inter[0][:, j % 2, m, :], h, ACT.Copy).then_inc(inter_high, 1)
                g, u = j // ST, j % ST
                if u < UNITS:
                    if u == 0:
                        act.wait_ge(d_done, pairs * (2 * ST * SUB) + (g * ST * SUB + D_CREDIT))
                    weight_high(pairs * (2 * UNITS) + ((g + 1) * UNITS + u), u, (g + 1) % 2)

            def tail(st):
                act.wait_ge(var_done, st + 1)
                act.activation(std[:, :], var_eps[:, :], ACT.Sqrt).then_inc(std_done, 1)

            steps(act, tail, body)

        @block.vector
        def _(dve):
            for t in range(ST):
                dve.sem_inc(out_stored[t], OUT_CREDIT)
            dve.sem_inc(u_done, U_CREDIT)
            dve.sem_inc(hid_done, HID_CREDIT)
            dve.sem_inc(inter_split, SPLIT_CREDIT)
            dve.sem_inc(d_added, ADD_CREDIT)
            dve.sem_inc(d_done, D_CREDIT)
            dve.sem_inc(w_made, W_CREDIT)
            dve.sem_inc(w_split, SPLITW_CREDIT)

            def unpack(number, loads, u, parity):
                step = number * 5
                dve.wait_ge(unit_loaded[parity], loads * 48)
                dve.wait_ge(w_made, number * 2 + W_CREDIT)
                raw = codes[:, parity, :]
                dve.tensor_scalar(bits_a[:, :], raw, 0xF0, 12, ALU.bitwise_and,
                                  ALU.logical_shift_left).then_inc(bit_step, 1)
                dve.wait_ge(bit_step, step + 1)
                dve.scalar_tensor_tensor(bits_b[:, :], raw, 0x0F, bits_a[:, :], ALU.bitwise_and,
                                         ALU.bitwise_or).then_inc(bit_step, 1)
                dve.wait_ge(bit_step, step + 2)
                dve.tensor_scalar(bits_a[:, :], bits_b[:, :], 0x00070007, 9, ALU.bitwise_and,
                                  ALU.logical_shift_left).then_inc(bit_step, 1)
                dve.tensor_scalar(bits_b[:, :], bits_b[:, :], 0x00080008, 12, ALU.bitwise_and,
                                  ALU.logical_shift_left).then_inc(bit_step, 1)
                dve.wait_ge(bit_step, step + 4)
                dve.tensor_tensor(bits_a[:, :], bits_a[:, :], bits_b[:, :], ALU.bitwise_or).then_inc(bit_step, 1)
                dve.wait_ge(bit_step, step + 5)
                value = bits_a[:, :].bitcast(F16).rearrange("p (n e) -> p e n", e=2)
                for n in range(2):
                    dve.wait_ge(w_split, number * 2 + (n + 1))
                    dve.scalar_tensor_tensor(w32[:, n, :], value[:, n, :], 2.0 ** 14, scale[:, parity, :],
                                             ALU.mult, ALU.mult).then_inc(w_made, 1)

            for u in range(UNITS):
                unpack(u, (1, 1, 2)[u], u, u % 2)

            def add_down(step, t, q):
                dve.wait_ge(d_done, step * SUB + (q + 1 + D_CREDIT))
                a = acc[:, t * SUB + q, :]
                dve.tensor_tensor(a, a, d_bank[q][:, :], ALU.add).then_inc(d_added, 1)

            def body(st, group, pairs, all_steps, j, first):
                for m in range(2):
                    use = (all_steps + j) * 2 + m
                    h = hid[:, m, :]
                    dve.wait_ge(square_done, use + 1)
                    dve.scalar_tensor_tensor(h, h, 1.0, g_bank[m][:, :], ALU.add, ALU.mult).then_inc(poly_done, 1)
                    for q in (2 * m, 2 * m + 1):
                        if not (first and j < 2):
                            if first and j < 6 and q == 0:
                                dve.wait_ge(acc_loaded[j - 2], st * 16 + 16)
                            add_down(all_steps + (j - 2), (j - 2) % ST, q)
                    dve.wait_ge(tanh_done, use + 1)
                    dve.scalar_tensor_tensor(h, h, 1.0, g_bank[m][:, :], ALU.add, ALU.mult).then_inc(gelu_done, 1)
                    dve.wait_ge(u_done, use + (1 + U_CREDIT))
                    dve.wait_ge(gelu_done, use + 1)
                    dve.scalar_tensor_tensor(h, h, 0.5, u_bank[m][:, :], ALU.mult, ALU.mult).then_inc(hid_done, 1)
                g, u = j // ST, j % ST
                if u < UNITS:
                    unit = (g + 1) * UNITS + u
                    unpack(pairs * (2 * UNITS) + unit, pairs * UNITS + (unit // 2 + 1), u, unit % 2)

            def tail(st):
                for j in (STEPS - 2, STEPS - 1):
                    for q in range(SUB):
                        add_down(st * STEPS + j, j % ST, q)
                n = SUPER // P
                dve.wait_ge(d_added, (st + 1) * (STEPS * SUB) + ADD_CREDIT)
                for a in range(n):
                    dve.bn_stats(stats[:, a, :], acc[:, a, :]).then_inc(stat_done, 1)
                for a in range(n):
                    wait_apart(dve, passed, stat_done, st * n + (a + 1))
                    dve.bn_aggr(mean_var[:, a, :], stats[:, a, :]).then_inc(agg_done, 1)
                dve.wait_ge(agg_done, st * n + n)
                dve.tensor_scalar(var_eps[:, :], mean_var[:, :, 1], EPS, None, ALU.add).then_inc(var_done, 1)
                dve.tensor_scalar(neg_mean[:, :], mean_var[:, :, 0], -1.0, None, ALU.mult)
                dve.wait_ge(std_done, st + 1)
                dve.reciprocal(rstd[:, :], std[:, :]).then_inc(rstd_done, 1)

            steps(dve, tail, body)

        @block.gpsimd
        def _(pool):
            def weight_low(number, u, w):
                for n in range(2):
                    pool.wait_ge(w_high, number * 2 + (n + 1))
                    pool.tensor_tensor(weight_part(1, u, w, n), half(w32[:, n, :], u),
                                       f32(weight_part(0, u, w, n)), ALU.subtract).then_inc(w_split, 1)

            for u in range(UNITS):
                weight_low(u, u, 0)

            def body(st, group, pairs, all_steps, j, first):
                for m in range(2):
                    pool.wait_ge(inter_high, (all_steps + j) * 2 + (m + 1))
                    pool.tensor_tensor(inter[1][:, j % 2, m, :], hid[:, m, :],
                                       f32(inter[0][:, j % 2, m, :]), ALU.subtract).then_inc(inter_split, 1)
                g, u = j // ST, j % ST
                if u < UNITS:
                    weight_low(pairs * (2 * UNITS) + ((g + 1) * UNITS + u), u, (g + 1) % 2)

            def tail(st):
                wait_apart(pool, passed, rstd_done, st + 1)
                for a in range(SUPER // P):
                    pool.tensor_scalar(acc[:, a, :], acc[:, a, :], neg_mean[:, a:a + 1], rstd[:, a:a + 1],
                                       ALU.add, ALU.mult).then_inc(out_made, 1)

            steps(pool, tail, body)


def program(nc, a, out):
    def internal(name, shape):
        return nc.dram_tensor(name, shape, F32, kind="Internal").ap()

    x1_dram = internal("x1_scratch", [TOK, HID])
    x1T_dram = internal("x1T_scratch", [2, HID, TOK])
    qk_dram = internal("qk_scratch", [2, 2, P, 2, SEQ])
    bank = [nc.alloc_psum_tensor(f"bank{i}", [P, 512], F32) for i in range(8)]
    attention_phase(nc, bank, a["xT"], a["x"], a["w_qkvT"], a["w_oT"], a["causal"], a["identity"],
                    x1_dram, x1T_dram, qk_dram)
    feed_forward_phase(nc, bank, x1_dram, x1T_dram, (a["gate"], a["up"], a["down"]),
                       (a["gate_scales"], a["up_scales"], a["down_scales"]), out)


def kernel(L0_attn_hidden_states, L0_attn_w_qkv, L0_attn_w_o, L0_ffn_gate_W_packed, L0_ffn_gate_scales,
           L0_ffn_up_W_packed, L0_ffn_up_scales, L0_ffn_down_W_packed, L0_ffn_down_scales):
    import numpy as np
    import concourse.bacc as bacc
    from concourse.bass_utils import run_bass_kernel_spmd

    def by_input(w):
        w = np.asarray(w)
        return np.ascontiguousarray(w.T.reshape(-1, MLP // GW, P, 2).transpose(0, 1, 3, 2).reshape(-1, MLP))

    x = np.ascontiguousarray(np.asarray(L0_attn_hidden_states).reshape(TOK, HID))
    causal = np.zeros((P, SEQ), np.float32)
    causal[:, SEQ - P:][np.triu_indices(P, 1)] = MASKED
    arrays = {
        "xT": np.ascontiguousarray(x.T),
        "x": x,
        "w_qkvT": np.ascontiguousarray(np.asarray(L0_attn_w_qkv).T),
        "w_oT": np.ascontiguousarray(np.asarray(L0_attn_w_o).T),
        "causal": causal,
        "identity": np.eye(P, dtype=np.float32),
        "gate": by_input(L0_ffn_gate_W_packed),
        "up": by_input(L0_ffn_up_W_packed),
        "down": np.ascontiguousarray(np.asarray(L0_ffn_down_W_packed).T),
        "gate_scales": by_input(L0_ffn_gate_scales),
        "up_scales": by_input(L0_ffn_up_scales),
        "down_scales": np.ascontiguousarray(np.asarray(L0_ffn_down_scales).T),
    }
    nc = bacc.Bacc("TRN2", target_bir_lowering=False, num_devices=1, dynamic_dma_scratch_size=1024)
    aps = {n: nc.dram_tensor(n, v.shape, mybir.dt.from_np(v.dtype), kind="ExternalInput").ap() for n, v in arrays.items()}
    out = nc.dram_tensor("out", [TOK, HID], F32, kind="ExternalOutput").ap()
    program(nc, aps, out)
    result = run_bass_kernel_spmd(nc, [arrays], core_ids=[0])
    return result.results[0]["out"].reshape(BATCH, SEQ, HID)
```
